# Optimizing a Trainium2 kernel written in Bass

```python
import numpy as np
import jax
import jax.numpy as jnp

def _softmax(x, axis=-1):
    return jax.nn.softmax(x, axis=axis)

def _gelu(x):
    return jax.nn.gelu(x, approximate=True)

def _silu(x):
    return jax.nn.silu(x)

def _sigmoid(x):
    return jax.nn.sigmoid(x)

def _layernorm(x, axis=-1, eps=1e-05):
    m = jnp.mean(x, axis=axis, keepdims=True)
    v = jnp.var(x, axis=axis, keepdims=True)
    return (x - m) / jnp.sqrt(v + eps)

def _scatter_add(tgt, idx, src, axis=0):
    return tgt.at[idx].add(src)

def _segment_sum(src, seg, n):
    return jax.ops.segment_sum(src, seg, n)
kernel_name = 'mk_adj_preln_d4_adj_r2_a688dd'

def setup_inputs(seed: int=0):
    np.random.seed(seed)
    _w = jnp.asarray

    def _rec_inputs():
        import jax
        import jax.numpy as jnp
        _gk = jax.random.key(seed)
        x = 7.34e-05 + 1 * jax.random.normal(jax.random.fold_in(_gk, 1), (128, 128, 256), jnp.float32)
        _a = jax.random.bernoulli(jax.random.fold_in(_gk, 2), 0.03125, (128, 128))
        _a = jnp.logical_or(_a, jnp.swapaxes(_a, -1, -2))
        _a = jnp.logical_or(_a, jnp.eye(128, dtype=bool))
        _af = _a.astype(jnp.float32)
        adj = _af
        return (x, adj)
    x, adj = _rec_inputs()

    def _L0_gnn_setup():
        import jax, jax.numpy as jnp
        import numpy as np
        B, N, D, H = (16, 1025, 256, 8)
        LN_EPS = 1e-05

        def _make_mask(key, n):
            n_proto = n - 1
            adj = jax.random.bernoulli(key, 0.03, (n_proto, n_proto)).astype(jnp.float32)
            adj = jnp.clip(adj + adj.T + jnp.eye(n_proto, dtype=jnp.float32), 0.0, 1.0)
            mask = jnp.zeros((n, n), dtype=jnp.float32)
            mask = mask.at[0, :].set(1.0).at[:, 0].set(1.0)
            mask = mask.at[1:, 1:].set(adj)
            return mask
        key = jax.random.key(seed)
        ks = jax.random.split(key, 7)
        s = 1.0 / np.sqrt(D)
        return {'x': jax.random.normal(ks[0], (B, N, D), dtype=jnp.float32), 'w_qkv': jax.random.uniform(ks[1], (D, 3 * D), dtype=jnp.float32, minval=-s, maxval=s), 'w_proj': jax.random.uniform(ks[2], (D, D), dtype=jnp.float32, minval=-s, maxval=s), 'b_proj': jnp.zeros((D,), dtype=jnp.float32), 'ln_gamma': jnp.ones((D,), dtype=jnp.float32), 'ln_beta': jnp.zeros((D,), dtype=jnp.float32), 'attn_mask': _make_mask(ks[3], N)}
    _L0_gnn_all = _L0_gnn_setup()
    _L0_gnn_in = {k: v for k, v in _L0_gnn_all.items() if k in ('w_qkv', 'w_proj', 'b_proj', 'ln_gamma', 'ln_beta')}
    del _L0_gnn_all

    def _L1_gnn_setup():
        import jax, jax.numpy as jnp
        import numpy as np
        B, N, D = (8, 1024, 256)
        key = jax.random.key(seed)
        k1, k2, k3, k4, k5 = jax.random.split(key, 5)
        neuron_states = jax.random.normal(k1, (B, N, D), dtype=jnp.float32)
        adjacency = jax.random.randint(k2, (N, N), 0, 2).astype(jnp.float32)
        scale = 1.0 / np.sqrt(D)
        Wq = jax.random.normal(k3, (D, D), dtype=jnp.float32) * scale
        Wk = jax.random.normal(k4, (D, D), dtype=jnp.float32) * scale
        Wv = jax.random.normal(k5, (D, D), dtype=jnp.float32) * scale
        return {'neuron_states': neuron_states, 'adjacency': adjacency, 'Wq': Wq, 'Wk': Wk, 'Wv': Wv}
    _L1_gnn_all = _L1_gnn_setup()
    _L1_gnn_in = {k: v for k, v in _L1_gnn_all.items() if k in ('Wq', 'Wk', 'Wv')}
    del _L1_gnn_all

    def _L2_gnn_setup():
        import jax, jax.numpy as jnp
        import numpy as np
        ALPHA = 0.2
        key = jax.random.key(seed)
        k0, k1, k2, k3 = jax.random.split(key, 4)
        B, N, C, F = (64, 512, 256, 256)
        x = jax.random.normal(k0, (B, N, C), dtype=jnp.float32)
        W = jax.random.normal(k1, (C, F), dtype=jnp.float32) * (1.414 / np.sqrt(C + F))
        a = jax.random.normal(k2, (2 * F, 1), dtype=jnp.float32) * (1.414 / np.sqrt(2 * F + 1))
        beta = jnp.ones((1,), dtype=jnp.float32)
        mask = (jax.random.uniform(k3, (N, N)) < 0.3).astype(jnp.float32)
        return {'x': x, 'W': W, 'a': a, 'beta': beta, 'mask': mask}
    _L2_gnn_all = _L2_gnn_setup()
    _L2_gnn_in = {k: v for k, v in _L2_gnn_all.items() if k in ('W', 'a', 'beta')}
    del _L2_gnn_all

    def _L3_gnn_setup():
        import jax, jax.numpy as jnp
        import numpy as np
        B, N, D, O = (8, 2048, 256, 256)
        key = jax.random.key(seed)
        k1, k2, k3, k4 = jax.random.split(key, 4)
        x = jax.random.normal(k1, (B, N, D), dtype=jnp.float32)
        adj = jax.random.uniform(k2, (N, N), dtype=jnp.float32)
        weight = jax.random.normal(k3, (D, O), dtype=jnp.float32) * 0.02
        bias = jax.random.normal(k4, (O,), dtype=jnp.float32) * 0.02
        return {'x': x, 'adj': adj, 'weight': weight, 'bias': bias}
    _L3_gnn_all = _L3_gnn_setup()
    _L3_gnn_in = {k: v for k, v in _L3_gnn_all.items() if k in ('weight', 'bias')}
    del _L3_gnn_all
    return {'x': x, 'adj': adj, 'L0_gnn_w_qkv': _L0_gnn_in['w_qkv'], 'L0_gnn_w_proj': _L0_gnn_in['w_proj'], 'L0_gnn_b_proj': _L0_gnn_in['b_proj'], 'L0_gnn_ln_gamma': _L0_gnn_in['ln_gamma'], 'L0_gnn_ln_beta': _L0_gnn_in['ln_beta'], 'L1_gnn_Wq': _L1_gnn_in['Wq'], 'L1_gnn_Wk': _L1_gnn_in['Wk'], 'L1_gnn_Wv': _L1_gnn_in['Wv'], 'L2_gnn_W': _L2_gnn_in['W'], 'L2_gnn_a': _L2_gnn_in['a'], 'L2_gnn_beta': _L2_gnn_in['beta'], 'L3_gnn_weight': _L3_gnn_in['weight'], 'L3_gnn_bias': _L3_gnn_in['bias']}

def reference(x, adj, L0_gnn_w_qkv, L0_gnn_w_proj, L0_gnn_b_proj, L0_gnn_ln_gamma, L0_gnn_ln_beta, L1_gnn_Wq, L1_gnn_Wk, L1_gnn_Wv, L2_gnn_W, L2_gnn_a, L2_gnn_beta, L3_gnn_weight, L3_gnn_bias):
    import jax
    import jax.numpy as jnp

    def _L0_gnn_ref(x, w_qkv, w_proj, b_proj, ln_gamma, ln_beta, attn_mask):
        import jax, jax.numpy as jnp
        import numpy as np
        B, N, D, H = (16, 1025, 256, 8)
        LN_EPS = 1e-05

        def _make_mask(key, n):
            n_proto = n - 1
            adj = jax.random.bernoulli(key, 0.03, (n_proto, n_proto)).astype(jnp.float32)
            adj = jnp.clip(adj + adj.T + jnp.eye(n_proto, dtype=jnp.float32), 0.0, 1.0)
            mask = jnp.zeros((n, n), dtype=jnp.float32)
            mask = mask.at[0, :].set(1.0).at[:, 0].set(1.0)
            mask = mask.at[1:, 1:].set(adj)
            return mask
        b, n, d = x.shape
        hd = d // H
        scale = hd ** (-0.5)
        qkv = (x @ w_qkv).reshape(b, n, 3, H, hd).transpose(2, 0, 3, 1, 4)
        q, k, v = (qkv[0], qkv[1], qkv[2])
        attn = jnp.einsum('bhnd,bhmd->bhnm', q, k) * scale
        attn = jnp.where(attn_mask[None, None] == 0, -jnp.inf, attn)
        attn = jax.nn.softmax(attn, axis=-1)
        o = jnp.einsum('bhnm,bhmd->bhnd', attn, v).transpose(0, 2, 1, 3).reshape(b, n, d)
        o = o @ w_proj + b_proj
        mu = jnp.mean(o, axis=-1, keepdims=True)
        var = jnp.mean(jnp.square(o - mu), axis=-1, keepdims=True)
        ln = (o - mu) * jax.lax.rsqrt(var + LN_EPS) * ln_gamma + ln_beta
        return o + ln

    def _L1_gnn_ref(neuron_states, adjacency, Wq, Wk, Wv):
        import jax, jax.numpy as jnp
        import numpy as np
        B, N, D = (8, 1024, 256)
        q = jnp.einsum('bnd,ed->bne', neuron_states, Wq)
        k = jnp.einsum('bnd,ed->bne', neuron_states, Wk)
        v = jnp.einsum('bnd,ed->bne', neuron_states, Wv)
        rel = jnp.einsum('bnd,bmd->bnm', q, k)
        rel = adjacency.T[None, :, :] * rel
        rel = rel / jnp.linalg.norm(rel, axis=2, keepdims=True)
        return jnp.einsum('bnm,bmd->bnd', rel, v)

    def _L2_gnn_ref(x, W, a, beta, mask):
        import jax, jax.numpy as jnp
        import numpy as np
        ALPHA = 0.2
        F_ = W.shape[1]
        h = jnp.einsum('bnc,cf->bnf', x, W)
        a1, a2 = (a[:F_, 0], a[F_:, 0])
        s1 = jnp.einsum('bnf,f->bn', h, a1)
        s2 = jnp.einsum('bnf,f->bn', h, a2)
        e = jax.nn.leaky_relu(s1[:, :, None] + s2[:, None, :], negative_slope=ALPHA)
        e = e * mask[None, :, :]
        att = jax.nn.softmax(e, axis=2)
        h_prime = jnp.einsum('bij,bjf->bif', att, h)
        return jax.nn.elu(h_prime + beta * h)

    def _L3_gnn_ref(x, adj, weight, bias):
        import jax, jax.numpy as jnp
        import numpy as np
        B, N, D, O = (8, 2048, 256, 256)
        y = jnp.einsum('nm,bmd->bnd', adj, x)
        out = jnp.einsum('bnd,do->bno', y, weight) + bias
        return out
    h = jnp.maximum(_layernorm(x, axis=-1), 0.0)
    x = x + _L0_gnn_ref(h, L0_gnn_w_qkv, L0_gnn_w_proj, L0_gnn_b_proj, L0_gnn_ln_gamma, L0_gnn_ln_beta, adj)
    h = jnp.maximum(_layernorm(x, axis=-1), 0.0)
    x = x + _L1_gnn_ref(h, adj, L1_gnn_Wq, L1_gnn_Wk, L1_gnn_Wv)
    h = jnp.maximum(_layernorm(x, axis=-1), 0.0)
    x = x + _L2_gnn_ref(h, L2_gnn_W, L2_gnn_a, L2_gnn_beta, adj)
    h = jnp.maximum(_layernorm(x, axis=-1), 0.0)
    x = x + _L3_gnn_ref(h, adj, L3_gnn_weight, L3_gnn_bias)
    return x

_drawn_inputs = setup_inputs


def setup_inputs(seed=0):
    import zlib

    import numpy as np

    out = dict(_drawn_inputs(seed))
    spreads = {'L0_gnn_b_proj': (0.0, 0.1), 'L0_gnn_ln_gamma': (1.0, 0.2), 'L0_gnn_ln_beta': (0.0, 0.1)}
    factors = {'L2_gnn_a': 8.0, 'L3_gnn_bias': 8.0}
    for name, (base, spread) in spreads.items():
        noise = np.random.default_rng([zlib.crc32(name.encode()), seed]).standard_normal(out[name].shape)
        drawn = base * np.exp(spread * noise) if base else spread * noise
        out[name] = jnp.asarray(drawn.astype(out[name].dtype))
    for name, factor in factors.items():
        out[name] = (out[name] * factor).astype(out[name].dtype)
    return out
```

```python
import numpy as np
import concourse.bass as bass
from concourse import mybir
from contextlib import ExitStack


def gnn_stack(nc, x, adj, adj_t, w_qkv, w_proj, b_proj, gamma, beta_ln, w_q, w_k, w_v_t,
              w_gat, w_gat_t, a_gat, beta_gat, w_out, b_out, out):
    f32 = mybir.dt.float32
    bf16 = mybir.dt.bfloat16
    ALU = mybir.AluOpType
    ACT = mybir.ActivationFunctionType
    AX = mybir.AxisListType

    B, N, D = x.shape
    H = 8
    HD = D // H
    C = D // 128
    PAIRS = B // 2
    RG = 128 // HD
    HC = H // RG
    W33 = HD + 1
    SCALE = float(HD) ** -0.5
    EPS = 1e-5
    MASKED = -1e30
    STREAMS = 4

    x_pairs = x.rearrange("(t b) n d -> t n b d", b=2)
    out_pairs = out.rearrange("(t b) n d -> t n b d", b=2)

    ctx = ExitStack()
    with ctx:
        def sb(name, shape, dt=f32):
            return ctx.enter_context(nc.sbuf_tensor(name, shape, dt))

        def sem(name):
            return ctx.enter_context(nc.semaphore(name))

        adj_sb = sb("adj_sb", [128, N])
        adj_t_sb = sb("adj_t_sb", [128, N])
        w_qkv_sb = sb("w_qkv_sb", [128, C, 3 * D])
        w_proj_sb = sb("w_proj_sb", [128, C, D])
        w_q_sb = sb("w_q_sb", [128, C, D])
        w_k_sb = sb("w_k_sb", [128, C, D])
        w_v_sb = sb("w_v_sb", [128, C, D])
        w_gat_sb = sb("w_gat_sb", [128, C, D])
        w_gat_t_sb = sb("w_gat_t_sb", [128, C, D])
        a_gat_sb = sb("a_gat_sb", [128, C, 2])
        w_out_sb = sb("w_out_sb", [128, C, D])
        b_proj_bc = sb("b_proj_bc", [128, D])
        gamma_bc = sb("gamma_bc", [128, D])
        beta_ln_bc = sb("beta_ln_bc", [128, D])
        b_out_bc = sb("b_out_bc", [128, D])
        beta_gat_bc = sb("beta_gat_bc", [128, 1])
        w_qk_sb = sb("w_qk_sb", [128, C, D])
        wa_sb = sb("wa_sb", [128, C, 2])
        ident = sb("ident", [128, 128])
        ident_b = sb("ident_b", [128, 128], bf16)
        mask_b = sb("mask_b", [128, N], bf16)
        ones = sb("ones", [128, 1])
        minus_half = sb("minus_half", [128, 2])
        eps = sb("eps", [128, 2])
        turn = sb("turn", [1, 1])

        x0 = sb("x0", [128, 2, 2, D])
        xb = sb("xb", [128, 2, 2, D])
        x1 = sb("x1", [128, 2, 2, D])
        x2 = sb("x2", [128, 2, 2, D])
        x3 = sb("x3", [128, 2, D])
        x3b = sb("x3b", [128, 2, D])
        x4 = sb("x4", [128, 2, 2, D])
        NORMS = 5
        LN_O = 4
        stats = sb("stats", [128, NORMS, 2, 6])
        mean_var = sb("mean_var", [128, NORMS, 2, 2])
        var_eps = sb("var_eps", [128, NORMS, 2])
        rstd = sb("rstd", [128, NORMS, 2])
        shift3 = sb("shift3", [128, 2])
        z = [sb(f"z{k}", [128, 2, D]) for k in range(3)]
        h_t = [sb(f"h_t{k}", [128, C, 2 * N]) for k in range(3)]
        q_t = sb("q_t", [128, HC, 2 * N])
        k_t = sb("k_t", [128, HC, 2 * N])
        v0 = sb("v0", [128, 2, H, W33])
        neg_max = sb("neg_max", [128, RG, 2 * HC])
        probs = sb("probs", [128, RG, 2 * HC, N])
        probs_t = sb("probs_t", [128, RG, 2 * HC, N])
        inv_sum = sb("inv_sum", [128, 2, H])
        o_heads = sb("o_heads", [128, 2, D])
        o_t = sb("o_t", [128, 2, C, N])
        o = sb("o", [128, 2, D])
        o_norm = sb("o_norm", [128, 2, D])
        o_res = sb("o_res", [128, 2, D])
        o_gam = sb("o_gam", [128, 2, D])
        g_t = sb("g_t", [128, C, 2 * N])
        v1 = sb("v1", [128, 2, D])
        rel = sb("rel", [128, 2, N])
        rel_sq = sb("rel_sq", [128, 2, N])
        sum_sq = sb("sum_sq", [128, 2])
        inv_norm = sb("inv_norm", [128, 2])
        hw = sb("hw", [128, 2, D])
        hw_beta = sb("hw_beta", [128, 2, D])
        s_sb = sb("s_sb", [128, 2, 2])
        e_sum = sb("e_sum", [128, 2, N])
        e_leaky = sb("e_leaky", [128, 2, N])
        e_mask = sb("e_mask", [128, 2, N])
        e_neg_max = sb("e_neg_max", [128, 2])
        att = sb("att", [128, 2, N])
        att_sum = sb("att_sum", [128, 2])
        att_inv = sb("att_inv", [128, 2])
        att_t = sb("att_t", [128, 2, N])
        u = sb("u", [128, 2, D])
        u_neg = sb("u_neg", [128, 2, D])
        u_exp = sb("u_exp", [128, 2, D])
        x2_neg = sb("x2_neg", [128, 2, D])
        h3 = sb("h3", [128, 2, D])
        y_t = sb("y_t", [128, C, 2 * N])

        mid = ctx.enter_context(nc.psum_tensor("mid", [128, RG, 512], f32))
        bank4 = ctx.enter_context(nc.psum_tensor("bank4", [128, 512], f32))
        bank5 = ctx.enter_context(nc.psum_tensor("bank5", [128, 512], f32))
        bank6 = ctx.enter_context(nc.psum_tensor("bank6", [128, 512], f32))
        bank7 = ctx.enter_context(nc.psum_tensor("bank7", [128, 512], f32))

        const_in = sem("const_in")
        x_in = [sem(f"x_in{i}") for i in range(2)]
        x_out = [sem(f"x_out{i}") for i in range(2)]
        idents_zeroed, ident_made, fills_made = sem("idents_zeroed"), sem("ident_made"), sem("fills_made")
        mask_made, folded, folded_copied = sem("mask_made"), sem("folded"), sem("folded_copied")
        ln_stats = [sem(f"ln_stats{k}") for k in range(NORMS)]
        ln_moments = [sem(f"ln_moments{k}") for k in range(NORMS)]
        ln_eps = [sem(f"ln_eps{k}") for k in range(NORMS)]
        ln_rstd = [sem(f"ln_rstd{k}") for k in range(NORMS)]
        z_ready = [sem(f"z_ready{k}") for k in range(3)]
        h_t_psum = [sem(f"h_t_psum{k}") for k in range(3)]
        h_t_ready = [sem(f"h_t_ready{k}") for k in range(3)]
        xb_ready = sem("xb_ready")
        q_psum, k_psum, v0_psum = sem("q_psum"), sem("k_psum"), sem("v0_psum")
        q_ready, k_ready, v0_ready = sem("q_ready"), sem("k_ready"), sem("v0_ready")
        scores_psum, max_ready = sem("scores_psum"), sem("max_ready")
        probs_ready, probs_t_psum, probs_t_ready = sem("probs_ready"), sem("probs_t_psum"), sem("probs_t_ready")
        heads_psum, inv_sum_ready, o_heads_ready = sem("heads_psum"), sem("inv_sum_ready"), sem("o_heads_ready")
        o_t_psum, o_t_ready, o_psum, o_ready = sem("o_t_psum"), sem("o_t_ready"), sem("o_psum"), sem("o_ready")
        o_norm_ready, o_res_ready, o_gam_ready, x1_ready = (
            sem("o_norm_ready"), sem("o_res_ready"), sem("o_gam_ready"), sem("x1_ready"))
        g_psum, g_ready, v1_psum, v1_ready = sem("g_psum"), sem("g_ready"), sem("v1_psum"), sem("v1_ready")
        rel_psum, rel_ready, rel_sq_ready = sem("rel_psum"), sem("rel_ready"), sem("rel_sq_ready")
        sum_sq_psum, sum_sq_ready, inv_norm_ready = sem("sum_sq_psum"), sem("sum_sq_ready"), sem("inv_norm_ready")
        rel_v_psum, x2_ready = sem("rel_v_psum"), sem("x2_ready")
        hw_psum, s_psum, s_ready, hw_ready, hw_beta_ready = (
            sem("hw_psum"), sem("s_psum"), sem("s_ready"), sem("hw_ready"), sem("hw_beta_ready"))
        s2_psum, e_sum_ready, e_leaky_ready, e_mask_ready, e_max_ready = (
            sem("s2_psum"), sem("e_sum_ready"), sem("e_leaky_ready"), sem("e_mask_ready"), sem("e_max_ready"))
        att_ready, att_inv_ready, att_t_psum, att_t_ready = (
            sem("att_ready"), sem("att_inv_ready"), sem("att_t_psum"), sem("att_t_ready"))
        att_h_psum, u_ready, u_neg_ready, u_exp_ready, x2_neg_ready, x3_ready, x3b_ready = (
            sem("att_h_psum"), sem("u_ready"), sem("u_neg_ready"), sem("u_exp_ready"),
            sem("x2_neg_ready"), sem("x3_ready"), sem("x3b_ready"))
        shift3_ready, h3_ready, y_t_psum, y_t_ready, y_psum, x4_ready = (
            sem("shift3_ready"), sem("h3_ready"), sem("y_t_psum"), sem("y_t_ready"), sem("y_psum"), sem("x4_ready"))

        block = ctx.enter_context(nc.Block())

        def done(p, n=1):
            return (p + 1) * n

        def wait_before(eng, s, p, n=1):
            if not isinstance(p, int) or p > 0:
                eng.wait_ge(s, p * n)

        def run(eng, step):
            def peeled(t):
                step(t, t % 2, [0 <= t - s < PAIRS for s in range(STREAMS)])
            for t in range(STREAMS):
                peeled(t)
            with eng.Fori(STREAMS, PAIRS - 1, 2) as t:
                step(t, 0, [True] * STREAMS)
                step(t + 1, 1, [True] * STREAMS)
            for t in range(PAIRS, PAIRS + STREAMS - 1):
                peeled(t)

        CONSTS = [
            (w_qkv_sb, w_qkv.rearrange("(c p) n -> p c n", p=128)),
            (adj_sb, adj), (adj_t_sb, adj_t),
            (w_q_sb, w_q.rearrange("(c p) n -> p c n", p=128)),
            (w_k_sb, w_k.rearrange("(c p) n -> p c n", p=128)),
            (w_gat_t_sb, w_gat_t.rearrange("(c p) n -> p c n", p=128)),
            (a_gat_sb, a_gat.rearrange("(c p) j -> p c j", p=128)),
            (w_proj_sb, w_proj.rearrange("(c p) n -> p c n", p=128)),
            (w_v_sb, w_v_t.rearrange("(c p) n -> p c n", p=128)),
            (w_gat_sb, w_gat.rearrange("(c p) n -> p c n", p=128)),
            (w_out_sb, w_out.rearrange("(c p) n -> p c n", p=128)),
            (b_proj_bc, b_proj.partition_broadcast(128)),
            (gamma_bc, gamma.partition_broadcast(128)),
            (beta_ln_bc, beta_ln.partition_broadcast(128)),
            (b_out_bc, b_out.partition_broadcast(128)),
            (beta_gat_bc, beta_gat.partition_broadcast(128)),
        ]
        ALL_CONSTS = 16 * len(CONSTS)

        @block.sync
        def _(sp):
            for i in range(2):
                sp.dma_start(x0[:, i], x_pairs[i]).then_inc(x_in[i], 16)
            for dst, src in CONSTS:
                sp.dma_start(dst[:], src).then_inc(const_in, 16)

            def step(t, par, on):
                p0, p3 = t, t - 3
                if on[0] and not (isinstance(t, int) and t + 2 >= PAIRS):
                    sp.wait_ge(z_ready[0], done(p0))
                    sp.wait_ge(xb_ready, done(p0))
                    sp.dma_start(x0[:, par], x_pairs[bass.ds(p0 + 2, 1)][0] if not isinstance(t, int)
                                 else x_pairs[t + 2]).then_inc(x_in[par], 16)
                if on[3]:
                    sp.wait_ge(x4_ready, done(p3))
                    sp.dma_start(out_pairs[bass.ds(p3, 1)][0] if not isinstance(t, int) else out_pairs[p3],
                                 x4[:, 1 - par]).then_inc(x_out[1 - par], 16)

            for t in range(STREAMS):
                step(t, t % 2, [True, True, True, t >= 3])
            with sp.Fori(STREAMS, PAIRS - 3, 2) as t:
                step(t, 0, [True] * STREAMS)
                step(t + 1, 1, [True] * STREAMS)
            for t in range(PAIRS - 2, PAIRS + STREAMS - 1):
                step(t, t % 2, [False, True, True, True])
            for i in range(2):
                sp.wait_ge(x_out[i], 16 * (PAIRS // 2))

        @block.tensor
        def _(pe):
            def transposes(dst, src, k):
                for b in range(2):
                    for c in range(C):
                        last = pe.transpose(dst[:, (c * 2 + b) * N:(c * 2 + b + 1) * N],
                                            src[:, b, c * 128:(c + 1) * 128], ident[:])
                last.then_inc(h_t_psum[k], 1)

            def rows(dst, lhs_t, w, signal):
                for b in range(2):
                    for c in range(C):
                        last = pe.matmul(dst[:, b * D:(b + 1) * D], lhs_t[:, c, b * N:(b + 1) * N], w[:, c, :],
                                         start=c == 0, stop=c == C - 1)
                last.then_inc(signal, 1)

            def columns(dst, w, w0, h, signal):
                for j in range(C):
                    for c in range(C):
                        last = pe.matmul(dst[:, j * 2 * N:(j + 1) * 2 * N],
                                         w[:, c, w0 + j * 128:w0 + (j + 1) * 128], h[:, c, :],
                                         start=c == 0, stop=c == C - 1)
                last.then_inc(signal, 1)

            pe.wait_ge(const_in, ALL_CONSTS)
            pe.wait_ge(ident_made, 2)
            pe.wait_ge(fills_made, 4)
            pe.wait_ge(mask_made, 1)
            for j in range(C):
                for c in range(C):
                    pe.matmul(bank4[:, j * D:(j + 1) * D], w_q_sb[:, c, j * 128:(j + 1) * 128], w_k_sb[:, c, :],
                              start=c == 0, stop=c == C - 1)
            for j in range(C):
                for c in range(C):
                    last = pe.matmul(bank5[:, j * 2:(j + 1) * 2], w_gat_t_sb[:, c, j * 128:(j + 1) * 128],
                                     a_gat_sb[:, c, :], start=c == 0, stop=c == C - 1)
            last.then_inc(folded, 1)
            pe.wait_ge(folded_copied, 2)

            def step(t, par, on):
                p0, p1, p2, p3 = t, t - 1, t - 2, t - 3
                front, middle, relation, gat = on
                peeled = isinstance(t, int)

                def transpose_probs(r):
                    pe.wait_ge(probs_ready, done(p1, RG) - (RG - 1 - r))
                    for s in range(2 * HC):
                        last = pe.transpose(mid[:, r, s * N:(s + 1) * N], probs[:, r, s], ident[:])
                    last.then_inc(probs_t_psum, 1)

                if middle:
                    pe.wait_ge(q_ready, done(p1))
                    pe.wait_ge(k_ready, done(p1))
                    wait_before(pe, o_heads_ready, p1)
                    wait_before(pe, o_t_ready, p1)
                    wait_before(pe, o_ready, p1)
                    for r in range(RG):
                        pe.matmul(mid[:, r], ident_b[:], mask_b[:].unsqueeze(1).to_broadcast([128, 2 * HC, N]),
                                  start=True, stop=True, skip_group_check=True)
                    for b in range(2):
                        for hc in range(HC):
                            for r in range(RG):
                                s = b * HC + hc
                                rows_r = slice(r * HD, (r + 1) * HD)
                                last = pe.matmul(mid[:, r, s * N:(s + 1) * N],
                                                 q_t[rows_r, hc, b * N:(b + 1) * N],
                                                 k_t[rows_r, hc, b * N:(b + 1) * N],
                                                 start=False, stop=True, tile_position=(r * HD, 0),
                                                 skip_group_check=True)
                    last.then_inc(scores_psum, 1)
                if gat:
                    pe.wait_ge(z_ready[2], done(p3))
                    wait_before(pe, y_t_ready, p3)
                    transposes(bank4, z[2], 2)
                if front:
                    pe.wait_ge(z_ready[0], done(p0))
                    if gat:
                        wait_before(pe, x4_ready, p3)
                    if relation and peeled:
                        wait_before(pe, x2_ready, p2, 2)
                    if peeled:
                        wait_before(pe, q_ready, p0)
                    transposes(bank6, z[0], 0)
                if gat:
                    pe.wait_ge(h_t_ready[2], done(p3))
                    if not peeled or t <= PAIRS:
                        wait_before(pe, v0_ready, p0)
                    else:
                        wait_before(pe, u_ready, p3)
                    rows(bank7, h_t[2], w_gat_sb, hw_psum)
                    for b in range(2):
                        for c in range(C):
                            last = pe.matmul(bank4[:, b * 2:(b + 1) * 2], h_t[2][:, c, b * N:(b + 1) * N],
                                             wa_sb[:, c, :], start=c == 0, stop=c == C - 1)
                    last.then_inc(s_psum, 1)
                if middle:
                    transpose_probs(0)
                if relation:
                    pe.wait_ge(z_ready[1], done(p2))
                    wait_before(pe, sum_sq_ready, p2)
                    transposes(bank5, z[1], 1)
                if front:
                    pe.wait_ge(h_t_ready[0], done(p0))
                    columns(bank6, w_qkv_sb, 0, h_t[0], q_psum)
                if gat:
                    pe.wait_ge(s_ready, done(p3))
                    for b in range(2):
                        last = pe.transpose(bank4[:, 256 + b * N:256 + (b + 1) * N],
                                            s_sb[:, b, 1:2].to_broadcast([128, 128]), ident[:])
                    last.then_inc(s2_psum, 1)
                if middle:
                    transpose_probs(1)
                if relation:
                    pe.wait_ge(h_t_ready[1], done(p2))
                    columns(bank5, w_qk_sb, 0, h_t[1], g_psum)
                if front:
                    if gat:
                        pe.wait_ge(hw_ready, done(p3))
                        pe.wait_ge(hw_beta_ready, done(p3))
                    else:
                        wait_before(pe, v0_ready, p0)
                    columns(bank7, w_qkv_sb, D, h_t[0], k_psum)
                if middle:
                    transpose_probs(2)
                if gat:
                    pe.wait_ge(att_ready, done(p3, 2))
                    for b in range(2):
                        last = pe.transpose(bank4[:, b * N:(b + 1) * N], att[:, b], ident[:])
                    last.then_inc(att_t_psum, 1)
                if relation:
                    if front:
                        pe.wait_ge(q_ready, done(p0))
                    else:
                        wait_before(pe, x4_ready, p3)
                    rows(bank6, h_t[1], w_v_sb, v1_psum)
                    pe.wait_ge(g_ready, done(p2))
                    for b in range(2):
                        for c in range(C):
                            last = pe.matmul(bank5[:, b * N:(b + 1) * N], h_t[1][:, c, b * N:(b + 1) * N],
                                             g_t[:, c, b * N:(b + 1) * N], start=c == 0, stop=c == C - 1)
                    last.then_inc(rel_psum, 1)
                if middle:
                    transpose_probs(3)
                if gat:
                    pe.wait_ge(att_t_ready, done(p3))
                    pe.wait_ge(hw_ready, done(p3))
                    if front:
                        pe.wait_ge(k_ready, done(p0))
                    else:
                        pe.wait_ge(hw_beta_ready, done(p3))
                    for b in range(2):
                        last = pe.matmul(bank7[:, b * D:(b + 1) * D], att_t[:, b], hw[:, b], start=True, stop=True)
                    last.then_inc(att_h_psum, 1)
                if middle:
                    pe.wait_ge(v0_ready, done(p1))
                    pe.wait_ge(probs_t_ready, done(p1, RG))
                    for b in range(2):
                        for h in range(H):
                            last = pe.matmul(mid[:, b, h * W33:(h + 1) * W33], probs_t[:, h % RG, b * HC + h // RG],
                                             v0[:, b, h], start=True, stop=True)
                    last.then_inc(heads_psum, 1)
                if relation:
                    pe.wait_ge(rel_sq_ready, done(p2))
                    for b in range(2):
                        last = pe.matmul(bank5[:, 256 + b:257 + b], rel_sq[:, b], ones[:], start=True, stop=True)
                    last.then_inc(sum_sq_psum, 1)
                    pe.wait_ge(v1_ready, done(p2))
                    for b in range(2):
                        last = pe.matmul(bank6[:, b * D:(b + 1) * D], rel[:, b], v1[:, b], start=True, stop=True)
                    last.then_inc(rel_v_psum, 1)
                if front:
                    if gat:
                        pe.wait_ge(u_ready, done(p3))
                    else:
                        pe.wait_ge(k_ready, done(p0))
                    rows(bank7, h_t[0], w_qkv_sb[:, :, 2 * D:3 * D], v0_psum)
                if middle:
                    pe.wait_ge(o_heads_ready, done(p1))
                    for b in range(2):
                        for c in range(C):
                            last = pe.transpose(mid[:, 2, (b * C + c) * N:(b * C + c + 1) * N],
                                                o_heads[:, b, c * 128:(c + 1) * 128], ident[:])
                    last.then_inc(o_t_psum, 1)
                    pe.wait_ge(o_t_ready, done(p1))
                    for b in range(2):
                        for c in range(C):
                            last = pe.matmul(mid[:, 3, b * D:(b + 1) * D], o_t[:, b, c], w_proj_sb[:, c, :],
                                             start=c == 0, stop=c == C - 1)
                    last.then_inc(o_psum, 1)
                if gat:
                    pe.wait_ge(h3_ready, done(p3))
                    for c in range(C):
                        for b in range(2):
                            last = pe.matmul(bank4[:, (c * 2 + b) * N:(c * 2 + b + 1) * N],
                                             h3[:, b, c * 128:(c + 1) * 128], adj_t_sb[:], start=True, stop=True)
                    last.then_inc(y_t_psum, 1)
                    pe.wait_ge(y_t_ready, done(p3))
                    if relation:
                        pe.wait_ge(x2_ready, done(p2, 2))
                    else:
                        wait_before(pe, x4_ready, p3)
                    rows(bank6, y_t, w_out_sb, y_psum)

            run(pe, step)

        @block.scalar
        def _(act):
            act.wait_ge(folded, 1)
            act.activation(w_qk_sb[:], bank4[:], ACT.Copy).then_inc(folded_copied, 1)
            act.activation(wa_sb[:], bank5[:, 0:2 * C], ACT.Copy).then_inc(folded_copied, 1)

            def step(t, par, on):
                p0, p1, p2, p3 = t, t - 1, t - 2, t - 3
                front, middle, relation, gat = on

                def relu_copy(k, p, bank):
                    act.wait_ge(h_t_psum[k], done(p))
                    act.activation(h_t[k][:], bank[:], ACT.Relu).then_inc(h_t_ready[k], 1)

                def exps(r):
                    if r % 2 == 0:
                        act.wait_ge(max_ready, done(p1, 2) - (1 - r // 2))
                    wait_before(act, probs_t_psum, p1, RG)
                    for s in range(2 * HC):
                        last = act.activation(probs[:, r, s], mid[:, r, s * N:(s + 1) * N], ACT.Exp,
                                              bias=neg_max[:, r, s:s + 1])
                    last.then_inc(probs_ready, 1)

                def copy_probs_t(r):
                    act.wait_ge(probs_t_psum, done(p1, RG) - (RG - 1 - r))
                    wait_before(act, heads_psum, p1)
                    act.activation(probs_t[:, r], mid[:, r], ACT.Copy).then_inc(probs_t_ready, 1)

                if gat:
                    relu_copy(2, p3, bank4)
                if front:
                    relu_copy(0, p0, bank6)
                if middle:
                    exps(0)
                if gat:
                    act.wait_ge(s_psum, done(p3))
                    act.activation(s_sb[:], bank4[:, 0:4], ACT.Copy).then_inc(s_ready, 1)
                    act.wait_ge(hw_psum, done(p3))
                    act.activation(hw[:], bank7[:], ACT.Copy).then_inc(hw_ready, 1)
                    act.activation(hw_beta[:], bank7[:], ACT.Identity, scale=beta_gat_bc[:]).then_inc(hw_beta_ready, 1)
                if middle:
                    exps(1)
                    copy_probs_t(0)
                if relation:
                    relu_copy(1, p2, bank5)
                if middle:
                    exps(2)
                if gat:
                    act.wait_ge(s2_psum, done(p3))
                    for b in range(2):
                        act.activation(e_sum[:, b], bank4[:, 256 + b * N:256 + (b + 1) * N], ACT.Identity,
                                       bias=s_sb[:, b, 0:1]).then_inc(e_sum_ready, 1)
                if front:
                    act.wait_ge(q_psum, done(p0))
                    act.activation(q_t[:], bank6[:], ACT.Copy, scale=SCALE).then_inc(q_ready, 1)
                if middle:
                    copy_probs_t(1)
                    exps(3)
                if relation:
                    act.wait_ge(g_psum, done(p2))
                    act.activation(g_t[:], bank5[:], ACT.Copy).then_inc(g_ready, 1)
                if front:
                    act.wait_ge(k_psum, done(p0))
                    act.activation(k_t[:], bank7[:], ACT.Copy).then_inc(k_ready, 1)
                if gat:
                    act.wait_ge(e_max_ready, done(p3))
                    for b in range(2):
                        act.activation(att[:, b], e_mask[:, b], ACT.Exp, bias=e_neg_max[:, b:b + 1],
                                       accum_out=att_sum[:, b:b + 1]).then_inc(att_ready, 1)
                if middle:
                    copy_probs_t(2)
                if gat:
                    act.wait_ge(att_t_psum, done(p3))
                    act.activation(att_t[:], bank4[:, 0:2 * N], ACT.Copy).then_inc(att_t_ready, 1)
                if relation:
                    act.wait_ge(v1_psum, done(p2))
                    act.activation(v1[:], bank6[:], ACT.Copy).then_inc(v1_ready, 1)
                if middle:
                    copy_probs_t(3)
                if gat:
                    act.wait_ge(u_neg_ready, done(p3))
                    act.activation(u_exp[:], u_neg[:], ACT.Exp).then_inc(u_exp_ready, 1)
                if front:
                    act.wait_ge(v0_psum, done(p0))
                    act.activation(v0[:, :, :, 0:HD], bank7[:].rearrange("p (b h d) -> p b h d", b=2, h=H),
                                   ACT.Copy).then_inc(v0_ready, 1)
                if middle:
                    act.wait_ge(o_t_psum, done(p1))
                    act.activation(o_t[:], mid[:, 2], ACT.Copy).then_inc(o_t_ready, 1)
                if gat:
                    act.wait_ge(shift3_ready, done(p3))
                    for b in range(2):
                        last = act.activation(h3[:, b], x3[:, b], ACT.Relu, bias=shift3[:, b:b + 1],
                                              scale=rstd[:, 3, b:b + 1])
                    last.then_inc(h3_ready, 1)
                    act.wait_ge(y_t_psum, done(p3))
                    act.activation(y_t[:], bank4[:], ACT.Copy).then_inc(y_t_ready, 1)

            run(act, step)

        @block.vector
        def _(dve):
            dve.wait_ge(const_in, ALL_CONSTS)
            dve.tensor_scalar(mask_b[:], adj_sb[:], 0.0, MASKED, ALU.is_equal, ALU.mult).then_inc(mask_made, 1)

            def moments(k, p, src):
                wait_before(dve, ln_rstd[k], p)
                for b in range(2):
                    dve.bn_stats(stats[:, k, b], src[:, b]).then_inc(ln_stats[k], 1)
                dve.wait_ge(ln_stats[k], done(p, 2))
                dve.memset(turn[:], 0.0)
                for b in range(2):
                    dve.bn_aggr(mean_var[:, k, b], stats[:, k, b]).then_inc(ln_moments[k], 1)

            def normalize(k, p, dst, src, signal):
                dve.wait_ge(ln_rstd[k], done(p))
                for b in range(2):
                    last = dve.tensor_scalar(dst[:, b], src[:, b], mean_var[:, k, b, 0:1], rstd[:, k, b:b + 1],
                                             ALU.subtract, ALU.mult)
                last.then_inc(signal, 1)

            def step(t, par, on):
                p0, p1, p2, p3 = t, t - 1, t - 2, t - 3
                front, middle, relation, gat = on

                if front:
                    dve.wait_ge(x_in[par], 8 * (p0 - par + 2))
                    moments(0, p0, x0[:, par])
                    wait_before(dve, h_t_psum[0], p0)
                    normalize(0, p0, z[0], x0[:, par], z_ready[0])
                if relation:
                    dve.wait_ge(x1_ready, done(p2))
                    moments(1, p2, x1[:, par])
                if middle:
                    dve.wait_ge(scores_psum, done(p1))
                    wait_before(dve, probs_ready, p1, RG)
                    dve.tensor_reduce(neg_max[:, 0:2], mid[:, 0:2].rearrange("p r (s m) -> p r s m", m=N),
                                      op=ALU.max, axis=AX.X, negate=True).then_inc(max_ready, 1)
                if relation:
                    wait_before(dve, h_t_psum[1], p2)
                    normalize(1, p2, z[1], x1[:, par], z_ready[1])
                if middle:
                    dve.tensor_reduce(neg_max[:, 2:4], mid[:, 2:4].rearrange("p r (s m) -> p r s m", m=N),
                                      op=ALU.max, axis=AX.X, negate=True).then_inc(max_ready, 1)
                if gat:
                    dve.wait_ge(e_sum_ready, done(p3, 2))
                    dve.scalar_tensor_tensor(e_leaky[:], e_sum[:], 0.2, e_sum[:], ALU.mult, ALU.max)\
                       .then_inc(e_leaky_ready, 1)
                    dve.wait_ge(e_mask_ready, done(p3))
                    wait_before(dve, att_ready, p3, 2)
                    dve.tensor_reduce(e_neg_max[:], e_mask[:], op=ALU.max, axis=AX.X, negate=True)\
                       .then_inc(e_max_ready, 1)
                    dve.wait_ge(att_ready, done(p3, 2))
                    dve.reciprocal(att_inv[:], att_sum[:]).then_inc(att_inv_ready, 1)
                if relation:
                    dve.wait_ge(rel_psum, done(p2))
                    wait_before(dve, rel_v_psum, p2)
                    dve.tensor_tensor(rel[:], bank5[:, 0:2 * N].rearrange("p (b n) -> p b n", b=2),
                                      adj_sb[:].unsqueeze(1).to_broadcast([128, 2, N]), ALU.mult)\
                       .then_inc(rel_ready, 1)
                if gat:
                    dve.wait_ge(att_h_psum, done(p3))
                    dve.wait_ge(att_inv_ready, done(p3))
                    dve.wait_ge(hw_beta_ready, done(p3))
                    for b in range(2):
                        last = dve.scalar_tensor_tensor(u[:, b], bank7[:, b * D:(b + 1) * D], att_inv[:, b:b + 1],
                                                        hw_beta[:, b], ALU.mult, ALU.add)
                    last.then_inc(u_ready, 1)
                    dve.wait_ge(u_ready, done(p3))
                    dve.tensor_scalar(u_neg[:], u[:], 0.0, None, ALU.min).then_inc(u_neg_ready, 1)
                if middle:
                    heads = mid[:, 0:2, 0:H * W33].rearrange("p b (h d) -> p b h d", h=H)
                    dve.wait_ge(heads_psum, done(p1))
                    dve.reciprocal(inv_sum[:], heads[:, :, :, HD]).then_inc(inv_sum_ready, 1)
                    dve.wait_ge(inv_sum_ready, done(p1))
                    wait_before(dve, o_t_psum, p1)
                    dve.tensor_tensor(o_heads[:].rearrange("p b (h d) -> p b h d", h=H), heads[:, :, :, 0:HD],
                                      inv_sum[:].unsqueeze(3).to_broadcast([128, 2, H, HD]), ALU.mult)\
                       .then_inc(o_heads_ready, 1)
                if gat:
                    dve.wait_ge(u_exp_ready, done(p3))
                    dve.scalar_tensor_tensor(x2_neg[:], u_exp[:], -1.0, x2[:, 1 - par], ALU.add, ALU.add)\
                       .then_inc(x2_neg_ready, 1)
                    dve.wait_ge(x2_neg_ready, done(p3))
                    dve.scalar_tensor_tensor(x3[:], u[:], 0.0, x2_neg[:], ALU.max, ALU.add).then_inc(x3_ready, 1)
                    dve.wait_ge(x3_ready, done(p3))
                    moments(3, p3, x3)
                if relation:
                    dve.wait_ge(sum_sq_psum, done(p2))
                    dve.tensor_copy(sum_sq[:], bank5[:, 256:258]).then_inc(sum_sq_ready, 1)
                    dve.wait_ge(rel_v_psum, done(p2))
                    dve.wait_ge(inv_norm_ready, done(p2))
                    for b in range(2):
                        dve.scalar_tensor_tensor(x2[:, par, b], bank6[:, b * D:(b + 1) * D], inv_norm[:, b:b + 1],
                                                 x1[:, par, b], ALU.mult, ALU.add).then_inc(x2_ready, 1)
                if gat:
                    dve.wait_ge(ln_rstd[3], done(p3))
                    dve.scalar_tensor_tensor(shift3[:], mean_var[:, 3, :, 0], -1.0, rstd[:, 3], ALU.mult, ALU.mult)\
                       .then_inc(shift3_ready, 1)
                if relation:
                    dve.wait_ge(x2_ready, done(p2, 2))
                    moments(2, p2, x2[:, par])
                if middle:
                    dve.wait_ge(o_psum, done(p1))
                    wait_before(dve, o_res_ready, p1)
                    dve.tensor_tensor(o[:], mid[:, 3].rearrange("p (b d) -> p b d", b=2),
                                      b_proj_bc[:].unsqueeze(1).to_broadcast([128, 2, D]), ALU.add)\
                       .then_inc(o_ready, 1)
                    dve.wait_ge(o_ready, done(p1))
                    moments(LN_O, p1, o)
                if relation:
                    wait_before(dve, h_t_psum[2], p2)
                    normalize(2, p2, z[2], x2[:, par], z_ready[2])
                if middle:
                    wait_before(dve, o_gam_ready, p1)
                    normalize(LN_O, p1, o_norm, o, o_norm_ready)
                if gat:
                    dve.wait_ge(y_psum, done(p3))
                    dve.wait_ge(x3b_ready, done(p3))
                    if not isinstance(t, int) or p3 > 1:
                        dve.wait_ge(x_out[1 - par], 8 * (p3 - (1 - par)))
                    dve.tensor_tensor(x4[:, 1 - par], bank6[:].rearrange("p (b d) -> p b d", b=2), x3b[:], ALU.add)\
                       .then_inc(x4_ready, 1)

            run(dve, step)

        @block.gpsimd
        def _(pool):
            for m in (ident, ident_b):
                pool.memset(m[:], 0.0).then_inc(idents_zeroed, 1)
            pool.memset(ones[:], 1.0).then_inc(fills_made, 1)
            pool.memset(minus_half[:], -0.5).then_inc(fills_made, 1)
            pool.memset(eps[:], EPS).then_inc(fills_made, 1)
            pool.memset(v0[:, :, :, HD:W33], 1.0).then_inc(fills_made, 1)
            pool.wait_ge(idents_zeroed, 2)
            for m in (ident, ident_b):
                pool.affine_select(out=m[:], in_=m[:], compare_op=ALU.not_equal, fill=1.0, base=0,
                                   pattern=[[-1, 128]], channel_multiplier=1).then_inc(ident_made, 1)
            pool.wait_ge(const_in, ALL_CONSTS)
            pool.wait_ge(fills_made, 4)

            def inverse_root(k, p):
                pool.wait_ge(ln_moments[k], done(p, 2))
                pool.tensor_tensor(var_eps[:, k], mean_var[:, k, :, 1], eps[:], ALU.add).then_inc(ln_eps[k], 1)
                pool.wait_ge(ln_eps[k], done(p))
                pool.tensor_tensor(rstd[:, k], var_eps[:, k], minus_half[:], ALU.pow).then_inc(ln_rstd[k], 1)

            def both(row):
                return row[:].unsqueeze(1).to_broadcast([128, 2, row.shape[-1]])

            def step(t, par, on):
                p0, p1, p2, p3 = t, t - 1, t - 2, t - 3
                front, middle, relation, gat = on

                if front:
                    wait_before(pool, z_ready[0], p0)
                    inverse_root(0, p0)
                    pool.wait_ge(x_in[par], 8 * (p0 - par + 2))
                    pool.tensor_tensor(xb[:, par], x0[:, par], both(beta_ln_bc), ALU.add).then_inc(xb_ready, 1)
                if relation:
                    wait_before(pool, z_ready[1], p2)
                    inverse_root(1, p2)
                if gat:
                    pool.wait_ge(e_leaky_ready, done(p3))
                    pool.tensor_tensor(e_mask[:], e_leaky[:], both(adj_sb), ALU.mult).then_inc(e_mask_ready, 1)
                if relation:
                    pool.wait_ge(rel_ready, done(p2))
                    wait_before(pool, sum_sq_psum, p2)
                    pool.tensor_tensor(rel_sq[:], rel[:], rel[:], ALU.mult).then_inc(rel_sq_ready, 1)
                if gat:
                    wait_before(pool, h3_ready, p3)
                    inverse_root(3, p3)
                    pool.wait_ge(x3_ready, done(p3))
                    wait_before(pool, x4_ready, p3)
                    pool.tensor_tensor(x3b[:], x3[:], both(b_out_bc), ALU.add).then_inc(x3b_ready, 1)
                if relation:
                    pool.wait_ge(sum_sq_ready, done(p2))
                    pool.tensor_tensor(inv_norm[:], sum_sq[:], minus_half[:], ALU.pow).then_inc(inv_norm_ready, 1)
                    wait_before(pool, z_ready[2], p2)
                    inverse_root(2, p2)
                if middle:
                    wait_before(pool, o_norm_ready, p1)
                    inverse_root(LN_O, p1)
                    pool.wait_ge(o_ready, done(p1))
                    pool.wait_ge(xb_ready, done(p1))
                    pool.tensor_tensor(o_res[:], o[:], xb[:, 1 - par], ALU.add).then_inc(o_res_ready, 1)
                    pool.wait_ge(o_norm_ready, done(p1))
                    pool.tensor_tensor(o_gam[:], o_norm[:], both(gamma_bc), ALU.mult).then_inc(o_gam_ready, 1)
                    pool.wait_ge(o_gam_ready, done(p1))
                    pool.wait_ge(o_res_ready, done(p1))
                    pool.tensor_tensor(x1[:, 1 - par], o_gam[:], o_res[:], ALU.add).then_inc(x1_ready, 1)

            run(pool, step)


def kernel(**inputs):
    import concourse.bacc as bacc
    from concourse.bass_utils import run_bass_kernel_spmd

    def laid(a):
        return np.ascontiguousarray(np.asarray(a))

    gat_w = inputs["L2_gnn_W"]
    arrays = {
        "x": laid(inputs["x"]),
        "adj": laid(inputs["adj"]),
        "adj_t": laid(np.asarray(inputs["adj"]).T),
        "w_qkv": laid(inputs["L0_gnn_w_qkv"]),
        "w_proj": laid(inputs["L0_gnn_w_proj"]),
        "b_proj": laid(inputs["L0_gnn_b_proj"]),
        "gamma": laid(inputs["L0_gnn_ln_gamma"]),
        "beta_ln": laid(inputs["L0_gnn_ln_beta"]),
        "w_q": laid(inputs["L1_gnn_Wq"]),
        "w_k": laid(inputs["L1_gnn_Wk"]),
        "w_v_t": laid(np.asarray(inputs["L1_gnn_Wv"]).T),
        "w_gat": laid(gat_w),
        "w_gat_t": laid(np.asarray(gat_w).T),
        "a_gat": laid(np.asarray(inputs["L2_gnn_a"]).reshape(2, -1).T),
        "beta_gat": laid(inputs["L2_gnn_beta"]),
        "w_out": laid(inputs["L3_gnn_weight"]),
        "b_out": laid(inputs["L3_gnn_bias"]),
    }
    nc = bacc.Bacc("TRN2", target_bir_lowering=False, num_devices=1)
    args = [nc.dram_tensor(f"in_{k}", a.shape, mybir.dt.from_np(a.dtype), kind="ExternalInput").ap()
            for k, a in arrays.items()]
    out = nc.dram_tensor("out_x", arrays["x"].shape, mybir.dt.float32, kind="ExternalOutput").ap()
    order = ["x", "adj", "adj_t", "w_qkv", "w_proj", "b_proj", "gamma", "beta_ln", "w_q", "w_k", "w_v_t",
             "w_gat", "w_gat_t", "a_gat", "beta_gat", "w_out", "b_out"]
    at = dict(zip(arrays, args))
    gnn_stack(nc, *[at[k] for k in order], out)
    r = run_bass_kernel_spmd(nc, [{f"in_{k}": a for k, a in arrays.items()}], core_ids=[0])
    return r.results[0]["out_x"]
```

```python
import numpy as np
import concourse.bass as bass
from concourse import mybir
from contextlib import ExitStack


def gnn_stack(nc, x, adj, adj_t, w_qkv, w_proj, b_proj, gamma, beta_ln, w_q, w_k, w_v_t,
              w_gat, a_gat, beta_gat, w_out, b_out, out):
    f32 = mybir.dt.float32
    f32r = mybir.dt.float32r
    bf16 = mybir.dt.bfloat16
    ALU = mybir.AluOpType
    ACT = mybir.ActivationFunctionType
    AX = mybir.AxisListType

    B, N, D = x.shape
    H = 8
    HD = D // H
    C = D // 128
    PAIRS = B // 2
    RG = 128 // HD
    HC = H // RG
    W33 = HD + 1
    SCALE = float(HD) ** -0.5
    EPS = 1e-5
    MASKED = -1e30
    STREAMS = 6

    x_pairs = x.rearrange("(t b) n d -> t n b d", b=2)
    out_pairs = out.rearrange("(t b) n d -> t n b d", b=2)

    ctx = ExitStack()
    with ctx:
        def sb(name, shape, dt=f32):
            return ctx.enter_context(nc.sbuf_tensor(name, shape, dt))

        def sem(name):
            return ctx.enter_context(nc.semaphore(name))

        def parts(name, shape):
            return [sb(f"{name}_{part}", shape, f32r) for part in ("hi", "lo")]

        adj_sb = sb("adj_sb", [128, N])
        adj_t_sb = sb("adj_t_sb", [128, N])
        w_qkv_sb = sb("w_qkv_sb", [128, C, 3 * D])
        w_proj_sb = sb("w_proj_sb", [128, C, D])
        w_q_sb = sb("w_q_sb", [128, C, D])
        w_k_sb = sb("w_k_sb", [128, C, D])
        w_v_sb = sb("w_v_sb", [128, C, D])
        w_gat_sb = sb("w_gat_sb", [128, C, D])
        w_out_sb = sb("w_out_sb", [128, C, D])
        w_qk_sb = sb("w_qk_sb", [128, C, D])
        w_qkv_p = parts("w_qkv", [128, C, 3 * D])
        w_proj_p = parts("w_proj", [128, C, D])
        w_v_p = parts("w_v", [128, C, D])
        w_gat_p = parts("w_gat", [128, C, D])
        w_out_p = parts("w_out", [128, C, D])
        w_qk_p = parts("w_qk", [128, C, D])
        a_gat_bc = sb("a_gat_bc", [128, 2, D])
        b_proj_bc = sb("b_proj_bc", [128, D])
        gamma_bc = sb("gamma_bc", [128, D])
        beta_ln_bc = sb("beta_ln_bc", [128, D])
        b_out_bc = sb("b_out_bc", [128, D])
        beta_gat_bc = sb("beta_gat_bc", [128, 1])
        ident = sb("ident", [128, 128])
        ident_b = sb("ident_b", [128, 128], bf16)
        mask_b = sb("mask_b", [128, N], bf16)
        ones = sb("ones", [128, 1])
        minus_half = sb("minus_half", [128, 2])
        eps = sb("eps", [128, 2])
        turn = sb("turn", [1, 1])

        x0 = sb("x0", [128, 2, 2, D])
        xb = sb("xb", [128, 2, 2, D])
        x1 = sb("x1", [128, 2, 2, D])
        x2 = sb("x2", [128, 2, 2, D])
        x3 = sb("x3", [128, 2, 2, D])
        x3b = sb("x3b", [128, 2, D])
        x4 = sb("x4", [128, 2, 2, D])
        NORMS = 5
        LN_O = 4
        stats = sb("stats", [128, NORMS, 2, 6])
        mean_var = sb("mean_var", [128, NORMS, 2, 2])
        var_eps = sb("var_eps", [128, NORMS, 2])
        rstd = sb("rstd", [128, NORMS, 2])
        shift3 = sb("shift3", [128, 2])
        z = [sb(f"z{k}", [128, 2, D]) for k in range(3)]
        h_t = [parts(f"h_t{k}", [128, C, 2 * N]) for k in range(3)]
        h_t1_full = sb("h_t1_full", [128, C, 2 * N])
        q_t = sb("q_t", [128, HC, 2 * N])
        k_diag = sb("k_diag", [128, HC, RG, 2 * N])
        v0 = sb("v0", [128, 2, 2, H, W33])
        BC = 2 * HC
        neg_max = sb("neg_max", [128, BC, RG])
        probs = sb("probs", [128, BC, RG, N])
        probs_t = sb("probs_t", [128, BC, RG, N])
        inv_sum = sb("inv_sum", [128, 2, H])
        o_heads = sb("o_heads", [128, 2, D])
        o_t = parts("o_t", [128, 2, C, N])
        o = sb("o", [128, 2, D])
        o_res = sb("o_res", [128, 2, D])
        o_gam = sb("o_gam", [128, 2, D])
        g_t = sb("g_t", [128, C, 2 * N])
        v1 = sb("v1", [128, 2, D])
        rel = sb("rel", [128, 2, N])
        rel_sq = sb("rel_sq", [128, 2, N])
        sum_sq = sb("sum_sq", [128, 2])
        inv_norm = sb("inv_norm", [128, 2])
        hw = sb("hw", [128, 2, D])
        hw_beta = sb("hw_beta", [128, 2, D])
        s_prod = sb("s_prod", [128, 2, 2, D])
        s_sb = sb("s_sb", [128, 2, 2])
        e_sum = sb("e_sum", [128, 2, N])
        e_leaky = sb("e_leaky", [128, 2, N])
        e_mask = sb("e_mask", [128, 2, N])
        e_neg_max = sb("e_neg_max", [128, 2])
        att = sb("att", [128, 2, N])
        att_sum = sb("att_sum", [128, 2])
        att_inv = sb("att_inv", [128, 2])
        att_t = sb("att_t", [128, 2, N])
        u = sb("u", [128, 2, D])
        u_neg = sb("u_neg", [128, 2, D])
        u_exp = sb("u_exp", [128, 2, D])
        x2_neg = sb("x2_neg", [128, 2, D])
        h3 = sb("h3", [128, 2, D])
        y_t = parts("y_t", [128, C, 2 * N])

        mid = ctx.enter_context(nc.psum_tensor("mid", [128, BC, 512], f32))
        bank4 = ctx.enter_context(nc.psum_tensor("bank4", [128, 512], f32))
        bank5 = ctx.enter_context(nc.psum_tensor("bank5", [128, 512], f32))
        bank6 = ctx.enter_context(nc.psum_tensor("bank6", [128, 512], f32))
        bank7 = ctx.enter_context(nc.psum_tensor("bank7", [128, 512], f32))

        const_in = sem("const_in")
        x_in = [sem(f"x_in{i}") for i in range(2)]
        x_out = [sem(f"x_out{i}") for i in range(2)]
        idents_zeroed, ident_made, fills_made = sem("idents_zeroed"), sem("ident_made"), sem("fills_made")
        mask_made, folded, folded_ready = sem("mask_made"), sem("folded"), sem("folded_ready")
        w_hi_ready, w_lo_ready = sem("w_hi_ready"), sem("w_lo_ready")
        ln_stats = [sem(f"ln_stats{k}") for k in range(NORMS)]
        ln_moments = [sem(f"ln_moments{k}") for k in range(NORMS)]
        ln_eps = [sem(f"ln_eps{k}") for k in range(NORMS)]
        ln_rstd = [sem(f"ln_rstd{k}") for k in range(NORMS)]
        z_ready = [sem(f"z_ready{k}") for k in range(3)]
        h_t_psum = [sem(f"h_t_psum{k}") for k in range(3)]
        h_hi_ready = [sem(f"h_hi_ready{k}") for k in range(3)]
        h_lo_ready = [sem(f"h_lo_ready{k}") for k in range(3)]
        xb_ready, h1_full_ready = sem("xb_ready"), sem("h1_full_ready")
        q_psum, k_psum, v0_psum = sem("q_psum"), sem("k_psum"), sem("v0_psum")
        q_ready, k_ready, v0_ready = sem("q_ready"), sem("k_ready"), sem("v0_ready")
        scores_psum, max_ready = sem("scores_psum"), sem("max_ready")
        probs_ready, probs_t_psum, probs_t_ready = sem("probs_ready"), sem("probs_t_psum"), sem("probs_t_ready")
        heads_psum, inv_sum_ready, o_heads_ready = sem("heads_psum"), sem("inv_sum_ready"), sem("o_heads_ready")
        o_t_psum, o_hi_ready, o_lo_ready = sem("o_t_psum"), sem("o_hi_ready"), sem("o_lo_ready")
        o_psum, o_ready = sem("o_psum"), sem("o_ready")
        o_res_ready, o_gam_ready, x1_ready = sem("o_res_ready"), sem("o_gam_ready"), sem("x1_ready")
        g_psum, g_ready, v1_psum, v1_ready = sem("g_psum"), sem("g_ready"), sem("v1_psum"), sem("v1_ready")
        rel_psum, rel_ready, rel_sq_ready = sem("rel_psum"), sem("rel_ready"), sem("rel_sq_ready")
        sum_sq_psum, sum_sq_ready, inv_norm_ready = sem("sum_sq_psum"), sem("sum_sq_ready"), sem("inv_norm_ready")
        rel_v_psum, x2_ready = sem("rel_v_psum"), sem("x2_ready")
        hw_psum, hw_ready, hw_beta_ready, s_ready = (
            sem("hw_psum"), sem("hw_ready"), sem("hw_beta_ready"), sem("s_ready"))
        s2_psum, e_sum_ready, e_leaky_ready, e_mask_ready, e_max_ready = (
            sem("s2_psum"), sem("e_sum_ready"), sem("e_leaky_ready"), sem("e_mask_ready"), sem("e_max_ready"))
        att_ready, att_inv_ready, att_t_psum, att_t_ready = (
            sem("att_ready"), sem("att_inv_ready"), sem("att_t_psum"), sem("att_t_ready"))
        att_h_psum, u_ready, u_neg_ready, u_exp_ready, x2_neg_ready, x3_ready, x3b_ready = (
            sem("att_h_psum"), sem("u_ready"), sem("u_neg_ready"), sem("u_exp_ready"),
            sem("x2_neg_ready"), sem("x3_ready"), sem("x3b_ready"))
        shift3_ready, h3_ready, y_t_psum, y_hi_ready, y_lo_ready, y_psum, x4_ready = (
            sem("shift3_ready"), sem("h3_ready"), sem("y_t_psum"), sem("y_hi_ready"), sem("y_lo_ready"),
            sem("y_psum"), sem("x4_ready"))

        block = ctx.enter_context(nc.Block())

        def done(p, n=1):
            return (p + 1) * n

        def wait_before(eng, s, p, n=1):
            if not isinstance(p, int) or p > 0:
                eng.wait_ge(s, p * n)

        def streams(t):
            return [0 <= t - s < PAIRS for s in range(STREAMS)]

        def run(eng, step):
            for t in range(STREAMS):
                step(t, t % 2, streams(t))
            with eng.Fori(STREAMS, PAIRS - 1, 2) as t:
                step(t, 0, [True] * STREAMS)
                step(t + 1, 1, [True] * STREAMS)
            for t in range(PAIRS, PAIRS + STREAMS - 1):
                step(t, t % 2, streams(t))

        def both(row):
            return row[:].unsqueeze(1).to_broadcast([128, 2, row.shape[-1]])

        CONSTS = [
            (adj_sb, adj),
            (w_q_sb, w_q.rearrange("(c p) n -> p c n", p=128)),
            (w_k_sb, w_k.rearrange("(c p) n -> p c n", p=128)),
            (w_qkv_sb, w_qkv.rearrange("(c p) n -> p c n", p=128)),
            (adj_t_sb, adj_t),
            (w_proj_sb, w_proj.rearrange("(c p) n -> p c n", p=128)),
            (w_v_sb, w_v_t.rearrange("(c p) n -> p c n", p=128)),
            (w_gat_sb, w_gat.rearrange("(c p) n -> p c n", p=128)),
            (w_out_sb, w_out.rearrange("(c p) n -> p c n", p=128)),
            (b_proj_bc, b_proj.partition_broadcast(128)),
            (gamma_bc, gamma.partition_broadcast(128)),
            (beta_ln_bc, beta_ln.partition_broadcast(128)),
            (b_out_bc, b_out.partition_broadcast(128)),
            (a_gat_bc, a_gat.partition_broadcast(128)),
            (beta_gat_bc, beta_gat.partition_broadcast(128)),
        ]
        ALL_CONSTS = 16 * len(CONSTS)
        SPLIT = [(w_qkv_sb, w_qkv_p), (w_proj_sb, w_proj_p), (w_v_sb, w_v_p), (w_gat_sb, w_gat_p),
                 (w_out_sb, w_out_p), (w_qk_sb, w_qk_p)]

        @block.sync
        def _(sp):
            for i in range(2):
                sp.dma_start(x0[:, i], x_pairs[i]).then_inc(x_in[i], 16)
            for dst, src in CONSTS:
                sp.dma_start(dst[:], src).then_inc(const_in, 16)

            def step(t, par, load, store):
                p1, p5 = t - 1, t - 5
                peeled = isinstance(t, int)
                if load:
                    sp.wait_ge(z_ready[0], done(p1))
                    sp.wait_ge(xb_ready, done(p1))
                    sp.dma_start(x0[:, 1 - par], x_pairs[p1 + 2] if peeled else x_pairs[bass.ds(p1 + 2, 1)][0])\
                      .then_inc(x_in[1 - par], 16)
                if store:
                    sp.wait_ge(x4_ready, done(p5))
                    sp.dma_start(out_pairs[p5] if peeled else out_pairs[bass.ds(p5, 1)][0],
                                 x4[:, 1 - par]).then_inc(x_out[1 - par], 16)

            for t in range(STREAMS):
                step(t, t % 2, t >= 1, t >= 5)
            with sp.Fori(STREAMS, PAIRS - 3, 2) as t:
                step(t, 0, True, True)
                step(t + 1, 1, True, True)
            for t in range(PAIRS - 2, PAIRS + STREAMS - 1):
                step(t, t % 2, t == PAIRS - 2, True)
            for i in range(2):
                sp.wait_ge(x_out[i], 16 * (PAIRS // 2))

        @block.tensor
        def _(pe):
            def product(dst, lhs_t, rhs, pick_l, pick_r):
                terms = [(c, a, b) for c in range(C) for a, b in ((0, 0), (0, 1), (1, 0))]
                for n, (c, a, b) in enumerate(terms):
                    last = pe.matmul(dst, pick_l(lhs_t[a], c), pick_r(rhs[b], c),
                                     start=n == 0, stop=n == len(terms) - 1)
                return last

            def transposes(dst, src, k):
                for b in range(2):
                    for c in range(C):
                        last = pe.transpose(dst[:, (c * 2 + b) * N:(c * 2 + b + 1) * N],
                                            src[:, b, c * 128:(c + 1) * 128], ident[:])
                last.then_inc(h_t_psum[k], 1)

            def rows(dst, h, w, w0, signal):
                for b in range(2):
                    last = product(dst[:, b * D:(b + 1) * D], h, w,
                                   lambda a, c: a[:, c, b * N:(b + 1) * N], lambda a, c: a[:, c, w0:w0 + D])
                last.then_inc(signal, 1)

            def columns(dst, w, w0, h, signal):
                for j in range(C):
                    last = product(dst[:, j * 2 * N:(j + 1) * 2 * N], w, h,
                                   lambda a, c: a[:, c, w0 + j * 128:w0 + (j + 1) * 128], lambda a, c: a[:, c])
                last.then_inc(signal, 1)

            pe.wait_ge(const_in, ALL_CONSTS)
            for j in range(C):
                for c in range(C):
                    last = pe.matmul(bank4[:, j * D:(j + 1) * D], w_q_sb[:, c, j * 128:(j + 1) * 128],
                                     w_k_sb[:, c, :], start=c == 0, stop=c == C - 1)
            last.then_inc(folded, 1)
            pe.wait_ge(ident_made, 2)
            pe.wait_ge(fills_made, 5)
            pe.wait_ge(mask_made, 1)
            pe.wait_ge(w_lo_ready, len(SPLIT))

            def step(t, par, on):
                p0, p1, p2, p3, p4, p5 = [t - s for s in range(STREAMS)]
                entry, front, middle, relation, gat, last_layer = on
                peeled = isinstance(t, int)
                on_before = streams(t - 1) if peeled else on

                def transpose_probs(s):
                    pe.wait_ge(probs_ready, done(p2, BC) - (BC - 1 - s))
                    for r in range(RG):
                        last = pe.transpose(mid[:, s, r * N:(r + 1) * N], probs[:, s, r], ident[:])
                    last.then_inc(probs_t_psum, 1)

                def heads_times_values(b):
                    pe.wait_ge(probs_t_ready, done(p2, BC) - HC * (1 - b))
                    for h in range(H):
                        last = pe.matmul(mid[:, b, h * W33:(h + 1) * W33], probs_t[:, b * HC + h // RG, h % RG],
                                         v0[:, par, b, h], start=True, stop=True)
                    last.then_inc(heads_psum, 1)

                if middle:
                    pe.wait_ge(q_ready, done(p2))
                    pe.wait_ge(k_ready, done(p2))
                    wait_before(pe, o_heads_ready, p2)
                    for b in range(2):
                        for hc in range(HC):
                            s = b * HC + hc
                            if s == 2:
                                wait_before(pe, o_lo_ready, p2)
                            if s == 3:
                                wait_before(pe, o_ready, p2)
                            pe.matmul(mid[:, s], ident_b[:], mask_b[:].unsqueeze(1).to_broadcast([128, RG, N]),
                                      start=True, stop=False)
                            last = pe.matmul(mid[:, s], q_t[:, hc, b * N:(b + 1) * N],
                                             k_diag[:, hc, :, b * N:(b + 1) * N], start=False, stop=True)
                            if s % 2 == 1:
                                last.then_inc(scores_psum, 1)
                if front:
                    pe.wait_ge(h_hi_ready[0], done(p1))
                    pe.wait_ge(h_lo_ready[0], done(p1))
                    if on_before[3]:
                        wait_before(pe, x2_ready, p3, 2)
                    elif on_before[1]:
                        wait_before(pe, k_ready, p1)
                    columns(bank6, w_qkv_p, 0, h_t[0], q_psum)
                if gat:
                    pe.wait_ge(z_ready[2], done(p4))
                    wait_before(pe, u_ready, p4)
                    transposes(bank4, z[2], 2)
                if middle:
                    transpose_probs(0)
                if last_layer:
                    pe.wait_ge(h3_ready, done(p5))
                    if on_before[0]:
                        pe.wait_ge(h_lo_ready[0], done(p1))
                    else:
                        wait_before(pe, x4_ready, p5)
                    for c in range(C):
                        for b in range(2):
                            last = pe.matmul(bank7[:, (c * 2 + b) * N:(c * 2 + b + 1) * N],
                                             h3[:, b, c * 128:(c + 1) * 128], adj_t_sb[:], start=True, stop=True)
                    last.then_inc(y_t_psum, 1)
                if front:
                    pe.wait_ge(q_ready, done(p1))
                    rows(bank6, h_t[0], w_qkv_p, 2 * D, v0_psum)
                if gat:
                    pe.wait_ge(h_hi_ready[2], done(p4))
                    pe.wait_ge(h_lo_ready[2], done(p4))
                    rows(bank4, h_t[2], w_gat_p, 0, hw_psum)
                if middle:
                    transpose_probs(1)
                if relation:
                    pe.wait_ge(z_ready[1], done(p3))
                    wait_before(pe, sum_sq_ready, p3)
                    transposes(bank5, z[1], 1)
                if last_layer:
                    pe.wait_ge(y_hi_ready, done(p5))
                    pe.wait_ge(y_lo_ready, done(p5))
                    rows(bank7, y_t, w_out_p, 0, y_psum)
                if front:
                    pe.wait_ge(v0_ready, done(p1))
                    columns(bank6, w_qkv_p, D, h_t[0], k_psum)
                if gat:
                    pe.wait_ge(s_ready, done(p4, 4))
                    pe.wait_ge(hw_beta_ready, done(p4))
                    for b in range(2):
                        last = pe.transpose(bank4[:, 256 + b * N:256 + (b + 1) * N],
                                            s_sb[:, b, 1:2].to_broadcast([128, 128]), ident[:])
                    last.then_inc(s2_psum, 1)
                if middle:
                    transpose_probs(2)
                if relation:
                    pe.wait_ge(h_hi_ready[1], done(p3))
                    pe.wait_ge(h_lo_ready[1], done(p3))
                    columns(bank5, w_qk_p, 0, h_t[1], g_psum)
                if middle:
                    transpose_probs(3)
                if relation:
                    pe.wait_ge(g_ready, done(p3))
                    for b in range(2):
                        for c in range(C):
                            last = pe.matmul(bank5[:, b * N:(b + 1) * N], h_t1_full[:, c, b * N:(b + 1) * N],
                                             g_t[:, c, b * N:(b + 1) * N], start=c == 0, stop=c == C - 1)
                    last.then_inc(rel_psum, 1)
                if gat:
                    pe.wait_ge(att_ready, done(p4, 2))
                    for b in range(2):
                        last = pe.transpose(bank4[:, b * N:(b + 1) * N], att[:, b], ident[:])
                    last.then_inc(att_t_psum, 1)
                if middle:
                    heads_times_values(0)
                if gat:
                    pe.wait_ge(att_t_ready, done(p4))
                    for b in range(2):
                        last = pe.matmul(bank4[:, b * D:(b + 1) * D], att_t[:, b], hw[:, b], start=True, stop=True)
                    last.then_inc(att_h_psum, 1)
                if middle:
                    heads_times_values(1)
                if relation:
                    if front:
                        pe.wait_ge(k_ready, done(p1))
                    elif on_before[3]:
                        wait_before(pe, x2_ready, p3, 2)
                    rows(bank6, h_t[1], w_v_p, 0, v1_psum)
                if middle:
                    pe.wait_ge(o_heads_ready, done(p2))
                    for b in range(2):
                        for c in range(C):
                            last = pe.transpose(mid[:, 2, (b * C + c) * N:(b * C + c + 1) * N],
                                                o_heads[:, b, c * 128:(c + 1) * 128], ident[:])
                    last.then_inc(o_t_psum, 1)
                if entry:
                    pe.wait_ge(z_ready[0], done(p0))
                    if last_layer:
                        pe.wait_ge(x4_ready, done(p5))
                    elif on_before[0]:
                        wait_before(pe, h_lo_ready[0], p0)
                    transposes(bank7, z[0], 0)
                if relation:
                    pe.wait_ge(v1_ready, done(p3))
                    pe.wait_ge(rel_ready, done(p3))
                    for b in range(2):
                        last = pe.matmul(bank6[:, b * D:(b + 1) * D], rel[:, b], v1[:, b], start=True, stop=True)
                    last.then_inc(rel_v_psum, 1)
                    pe.wait_ge(rel_sq_ready, done(p3))
                    for b in range(2):
                        last = pe.matmul(bank5[:, 256 + b:257 + b], rel_sq[:, b], ones[:], start=True, stop=True)
                    last.then_inc(sum_sq_psum, 1)
                if middle:
                    pe.wait_ge(o_hi_ready, done(p2))
                    pe.wait_ge(o_lo_ready, done(p2))
                    for b in range(2):
                        last = product(mid[:, 3, b * D:(b + 1) * D], o_t, w_proj_p,
                                       lambda a, c: a[:, b, c], lambda a, c: a[:, c])
                    last.then_inc(o_psum, 1)

            run(pe, step)

        @block.scalar
        def _(act):
            act.wait_ge(const_in, ALL_CONSTS)
            for w, (hi, _) in SPLIT[:-1]:
                act.activation(hi[:], w[:], ACT.Copy).then_inc(w_hi_ready, 1)
            act.wait_ge(folded, 1)
            act.activation(w_qk_sb[:], bank4[:], ACT.Copy).then_inc(folded_ready, 1)
            act.activation(w_qk_p[0][:], bank4[:], ACT.Copy).then_inc(w_hi_ready, 1)

            def step(t, par, on):
                p0, p1, p2, p3, p4, p5 = [t - s for s in range(STREAMS)]
                entry, front, middle, relation, gat, last_layer = on

                def relu_hi(k, p, bank, users):
                    act.wait_ge(h_t_psum[k], done(p))
                    for psum in users:
                        wait_before(act, psum, p)
                    act.activation(h_t[k][0][:], bank[:], ACT.Relu).then_inc(h_hi_ready[k], 1)

                def exps(s):
                    if s % 2 == 0:
                        act.wait_ge(max_ready, done(p2, 2) - (1 - s // 2))
                    wait_before(act, probs_t_psum, p2, BC)
                    for r in range(RG):
                        last = act.activation(probs[:, s, r], mid[:, s, r * N:(r + 1) * N], ACT.Exp,
                                              bias=neg_max[:, s, r:r + 1])
                    last.then_inc(probs_ready, 1)

                def copy_probs_t(s):
                    act.wait_ge(probs_t_psum, done(p2, BC) - (BC - 1 - s))
                    wait_before(act, heads_psum, p2, 2)
                    act.activation(probs_t[:, s], mid[:, s], ACT.Copy).then_inc(probs_t_ready, 1)

                if middle:
                    exps(0)
                if middle:
                    exps(1)
                if front:
                    act.wait_ge(q_psum, done(p1))
                    act.activation(q_t[:], bank6[:], ACT.Copy, scale=SCALE).then_inc(q_ready, 1)
                if gat:
                    relu_hi(2, p4, bank4, [hw_psum])
                if middle:
                    copy_probs_t(0)
                if last_layer:
                    act.wait_ge(y_t_psum, done(p5))
                    wait_before(act, y_psum, p5)
                    act.activation(y_t[0][:], bank7[:], ACT.Copy).then_inc(y_hi_ready, 1)
                if middle:
                    exps(2)
                if front:
                    act.wait_ge(v0_psum, done(p1))
                    act.activation(v0[:, 1 - par, :, :, 0:HD], bank6[:].rearrange("p (b h d) -> p b h d", b=2, h=H),
                                   ACT.Copy).then_inc(v0_ready, 1)
                if middle:
                    exps(3)
                if gat:
                    act.wait_ge(hw_psum, done(p4))
                    act.activation(hw[:], bank4[:], ACT.Copy).then_inc(hw_ready, 1)
                if gat:
                    act.activation(hw_beta[:], bank4[:], ACT.Identity, scale=beta_gat_bc[:]).then_inc(hw_beta_ready, 1)
                if middle:
                    copy_probs_t(1)
                if relation:
                    relu_hi(1, p3, bank5, [v1_psum])
                    wait_before(act, rel_psum, p3)
                    act.activation(h_t1_full[:], bank5[:], ACT.Relu).then_inc(h1_full_ready, 1)
                if gat:
                    act.wait_ge(s2_psum, done(p4))
                    for b in range(2):
                        act.activation(e_sum[:, b], bank4[:, 256 + b * N:256 + (b + 1) * N], ACT.Identity,
                                       bias=s_sb[:, b, 0:1]).then_inc(e_sum_ready, 1)
                if middle:
                    copy_probs_t(2)
                if relation:
                    act.wait_ge(g_psum, done(p3))
                    act.activation(g_t[:], bank5[:], ACT.Copy).then_inc(g_ready, 1)
                if gat:
                    act.wait_ge(e_max_ready, done(p4))
                    wait_before(act, att_inv_ready, p4)
                    for b in range(2):
                        act.activation(att[:, b], e_mask[:, b], ACT.Exp, bias=e_neg_max[:, b:b + 1],
                                       accum_out=att_sum[:, b:b + 1]).then_inc(att_ready, 1)
                if middle:
                    copy_probs_t(3)
                if gat:
                    act.wait_ge(att_t_psum, done(p4))
                    act.activation(att_t[:], bank4[:, 0:2 * N], ACT.Copy).then_inc(att_t_ready, 1)
                if front:
                    act.wait_ge(k_psum, done(p1))
                    for r in range(RG):
                        at = slice(r * HD, (r + 1) * HD)
                        last = act.activation(k_diag[at, :, r, :], bank6[at, :].rearrange("p (h n) -> p h n", h=HC),
                                              ACT.Copy)
                    last.then_inc(k_ready, 1)
                if gat:
                    act.wait_ge(u_neg_ready, done(p4))
                    act.activation(u_exp[:], u_neg[:], ACT.Exp).then_inc(u_exp_ready, 1)
                if relation:
                    act.wait_ge(v1_psum, done(p3))
                    act.activation(v1[:], bank6[:], ACT.Copy).then_inc(v1_ready, 1)
                if middle:
                    act.wait_ge(o_t_psum, done(p2))
                    act.activation(o_t[0][:], mid[:, 2], ACT.Copy).then_inc(o_hi_ready, 1)
                if entry:
                    relu_hi(0, p0, bank7, [k_psum])
                if gat:
                    act.wait_ge(shift3_ready, done(p4))
                    wait_before(act, y_t_psum, p4)
                    for b in range(2):
                        last = act.activation(h3[:, b], x3[:, par, b], ACT.Relu, bias=shift3[:, b:b + 1],
                                              scale=rstd[:, 3, b:b + 1])
                    last.then_inc(h3_ready, 1)

            run(act, step)

        @block.vector
        def _(dve):
            dve.wait_ge(const_in, ALL_CONSTS)
            dve.tensor_scalar(mask_b[:], adj_sb[:], 0.0, MASKED, ALU.is_equal, ALU.mult).then_inc(mask_made, 1)
            for n, (w, (hi, lo)) in enumerate(SPLIT):
                dve.wait_ge(w_hi_ready, n + 1)
                if w is w_qk_sb:
                    dve.wait_ge(folded_ready, 1)
                dve.tensor_tensor(lo[:], w[:], hi[:].bitcast(f32), ALU.subtract).then_inc(w_lo_ready, 1)

            def moments(k, p, src):
                wait_before(dve, ln_rstd[k], p)
                for b in range(2):
                    dve.bn_stats(stats[:, k, b], src[:, b]).then_inc(ln_stats[k], 1)
                dve.wait_ge(ln_stats[k], done(p, 2))
                dve.memset(turn[:], 0.0)
                for b in range(2):
                    dve.bn_aggr(mean_var[:, k, b], stats[:, k, b]).then_inc(ln_moments[k], 1)

            def normalize(k, p, dst, src, signal):
                dve.wait_ge(ln_rstd[k], done(p))
                for b in range(2):
                    last = dve.tensor_scalar(dst[:, b], src[:, b], mean_var[:, k, b, 0:1], rstd[:, k, b:b + 1],
                                             ALU.subtract, ALU.mult)
                last.then_inc(signal, 1)

            def relu_lo(k, p, bank):
                dve.wait_ge(h_hi_ready[k], done(p))
                dve.scalar_tensor_tensor(h_t[k][1][:].rearrange("p c n -> p (c n)"), bank[:], 0.0,
                                         h_t[k][0][:].rearrange("p c n -> p (c n)").bitcast(f32),
                                         ALU.max, ALU.subtract).then_inc(h_lo_ready[k], 1)

            def step(t, par, on):
                p0, p1, p2, p3, p4, p5 = [t - s for s in range(STREAMS)]
                entry, front, middle, relation, gat, last_layer = on

                def maxima(half):
                    dve.wait_ge(scores_psum, done(p2, 2) - (1 - half))
                    if half == 0:
                        wait_before(dve, probs_ready, p2, BC)
                    at = slice(2 * half, 2 * half + 2)
                    dve.tensor_reduce(neg_max[:, at], mid[:, at].rearrange("p s (r m) -> p s r m", m=N),
                                      op=ALU.max, axis=AX.X, negate=True).then_inc(max_ready, 1)

                if middle:
                    maxima(0)
                if gat:
                    wait_before(dve, h_t_psum[2], p4)
                    normalize(2, p4, z[2], x2[:, par], z_ready[2])
                if relation:
                    dve.wait_ge(ln_moments[LN_O], done(p3, 2))
                    for b in range(2):
                        last = dve.scalar_tensor_tensor(o_gam[:, b], o[:, b], mean_var[:, LN_O, b, 0:1], gamma_bc[:],
                                                        ALU.subtract, ALU.mult)
                    last.then_inc(o_gam_ready, 1)
                    dve.wait_ge(o_gam_ready, done(p3))
                    dve.wait_ge(ln_rstd[LN_O], done(p3))
                    dve.wait_ge(o_res_ready, done(p3))
                    for b in range(2):
                        dve.scalar_tensor_tensor(x1[:, 1 - par, b], o_gam[:, b], rstd[:, LN_O, b:b + 1], o_res[:, b],
                                                 ALU.mult, ALU.add).then_inc(x1_ready, 1)
                if middle:
                    maxima(1)
                if gat:
                    relu_lo(2, p4, bank4)
                if relation:
                    dve.wait_ge(x1_ready, done(p3, 2))
                    moments(1, p3, x1[:, 1 - par])
                if last_layer:
                    dve.wait_ge(y_hi_ready, done(p5))
                    dve.tensor_tensor(y_t[1][:].rearrange("p c n -> p (c n)"), bank7[:],
                                      y_t[0][:].rearrange("p c n -> p (c n)").bitcast(f32), ALU.subtract)\
                       .then_inc(y_lo_ready, 1)
                if relation:
                    wait_before(dve, h_t_psum[1], p3)
                    normalize(1, p3, z[1], x1[:, 1 - par], z_ready[1])
                if gat:
                    dve.wait_ge(hw_ready, done(p4))
                    wait_before(dve, s2_psum, p4)
                    for b in range(2):
                        for j in range(2):
                            dve.tensor_tensor_reduce(out=s_prod[:, b, j], in0=hw[:, b], in1=a_gat_bc[:, j],
                                                     scale=1.0, scalar=0.0, op0=ALU.mult, op1=ALU.add,
                                                     accum_out=s_sb[:, b, j:j + 1]).then_inc(s_ready, 1)
                if last_layer:
                    dve.wait_ge(y_psum, done(p5))
                    dve.wait_ge(x3b_ready, done(p5))
                    if not isinstance(t, int) or p5 > 1:
                        dve.wait_ge(x_out[1 - par], 8 * (p5 - (1 - par)))
                    dve.tensor_tensor(x4[:, 1 - par], bank7[:].rearrange("p (b d) -> p b d", b=2), x3b[:], ALU.add)\
                       .then_inc(x4_ready, 1)
                if entry:
                    dve.wait_ge(x_in[par], 8 * (p0 - par + 2))
                    moments(0, p0, x0[:, par])
                if gat:
                    dve.wait_ge(e_sum_ready, done(p4, 2))
                    dve.scalar_tensor_tensor(e_leaky[:], e_sum[:], 0.2, e_sum[:], ALU.mult, ALU.max)\
                       .then_inc(e_leaky_ready, 1)
                if entry:
                    wait_before(dve, h_t_psum[0], p0)
                    normalize(0, p0, z[0], x0[:, par], z_ready[0])
                if gat:
                    dve.wait_ge(e_mask_ready, done(p4))
                    wait_before(dve, att_ready, p4, 2)
                    dve.tensor_reduce(e_neg_max[:], e_mask[:], op=ALU.max, axis=AX.X, negate=True)\
                       .then_inc(e_max_ready, 1)
                    dve.wait_ge(att_ready, done(p4, 2))
                    dve.reciprocal(att_inv[:], att_sum[:]).then_inc(att_inv_ready, 1)
                if relation:
                    dve.wait_ge(rel_psum, done(p3))
                    wait_before(dve, rel_v_psum, p3)
                    dve.tensor_tensor(rel[:], bank5[:, 0:2 * N].rearrange("p (b n) -> p b n", b=2),
                                      both(adj_sb), ALU.mult).then_inc(rel_ready, 1)
                if gat:
                    dve.wait_ge(att_h_psum, done(p4))
                    dve.wait_ge(att_inv_ready, done(p4))
                    dve.wait_ge(hw_beta_ready, done(p4))
                    for b in range(2):
                        last = dve.scalar_tensor_tensor(u[:, b], bank4[:, b * D:(b + 1) * D], att_inv[:, b:b + 1],
                                                        hw_beta[:, b], ALU.mult, ALU.add)
                    last.then_inc(u_ready, 1)
                    dve.wait_ge(u_ready, done(p4))
                    dve.tensor_scalar(u_neg[:], u[:], 0.0, None, ALU.min).then_inc(u_neg_ready, 1)
                    dve.wait_ge(u_exp_ready, done(p4))
                    dve.scalar_tensor_tensor(x2_neg[:], u_exp[:], -1.0, x2[:, par], ALU.add, ALU.add)\
                       .then_inc(x2_neg_ready, 1)
                    dve.wait_ge(x2_neg_ready, done(p4))
                    dve.scalar_tensor_tensor(x3[:, par], u[:], 0.0, x2_neg[:], ALU.max, ALU.add).then_inc(x3_ready, 1)
                if middle:
                    heads = mid[:, 0:2, 0:H * W33].rearrange("p b (h d) -> p b h d", h=H)
                    dve.wait_ge(heads_psum, done(p2, 2))
                    dve.reciprocal(inv_sum[:], heads[:, :, :, HD]).then_inc(inv_sum_ready, 1)
                    dve.wait_ge(inv_sum_ready, done(p2))
                    wait_before(dve, o_t_psum, p2)
                    dve.tensor_tensor(o_heads[:].rearrange("p b (h d) -> p b h d", h=H), heads[:, :, :, 0:HD],
                                      inv_sum[:].unsqueeze(3).to_broadcast([128, 2, H, HD]), ALU.mult)\
                       .then_inc(o_heads_ready, 1)
                    dve.wait_ge(o_hi_ready, done(p2))
                    wait_before(dve, o_psum, p2)
                    dve.tensor_tensor(o_t[1][:].rearrange("p b c n -> p (b c n)"), mid[:, 2],
                                      o_t[0][:].rearrange("p b c n -> p (b c n)").bitcast(f32), ALU.subtract)\
                       .then_inc(o_lo_ready, 1)
                if relation:
                    dve.wait_ge(sum_sq_psum, done(p3))
                    dve.tensor_copy(sum_sq[:], bank5[:, 256:258]).then_inc(sum_sq_ready, 1)
                if entry:
                    relu_lo(0, p0, bank7)
                if gat:
                    dve.wait_ge(x3_ready, done(p4))
                    moments(3, p4, x3[:, par])
                if relation:
                    dve.wait_ge(rel_v_psum, done(p3))
                    dve.wait_ge(inv_norm_ready, done(p3))
                    for b in range(2):
                        dve.scalar_tensor_tensor(x2[:, 1 - par, b], bank6[:, b * D:(b + 1) * D], inv_norm[:, b:b + 1],
                                                 x1[:, 1 - par, b], ALU.mult, ALU.add).then_inc(x2_ready, 1)
                if gat:
                    dve.wait_ge(ln_rstd[3], done(p4))
                    wait_before(dve, h3_ready, p4)
                    dve.scalar_tensor_tensor(shift3[:], mean_var[:, 3, :, 0], -1.0, rstd[:, 3], ALU.mult, ALU.mult)\
                       .then_inc(shift3_ready, 1)
                if middle:
                    dve.wait_ge(o_psum, done(p2))
                    wait_before(dve, o_res_ready, p2)
                    dve.tensor_tensor(o[:], mid[:, 3].rearrange("p (b d) -> p b d", b=2), both(b_proj_bc), ALU.add)\
                       .then_inc(o_ready, 1)
                if relation:
                    dve.wait_ge(x2_ready, done(p3, 2))
                    moments(2, p3, x2[:, 1 - par])
                if middle:
                    dve.wait_ge(o_ready, done(p2))
                    moments(LN_O, p2, o)

            run(dve, step)

        @block.gpsimd
        def _(pool):
            for m in (ident, ident_b):
                pool.memset(m[:], 0.0).then_inc(idents_zeroed, 1)
            pool.memset(ones[:], 1.0).then_inc(fills_made, 1)
            pool.memset(minus_half[:], -0.5).then_inc(fills_made, 1)
            pool.memset(eps[:], EPS).then_inc(fills_made, 1)
            pool.memset(v0[:, :, :, :, HD:W33], 1.0).then_inc(fills_made, 1)
            pool.memset(k_diag[:], 0.0).then_inc(fills_made, 1)
            pool.wait_ge(idents_zeroed, 2)
            for m in (ident, ident_b):
                pool.affine_select(out=m[:], in_=m[:], compare_op=ALU.not_equal, fill=1.0, base=0,
                                   pattern=[[-1, 128]], channel_multiplier=1).then_inc(ident_made, 1)
            pool.wait_ge(const_in, ALL_CONSTS)
            pool.wait_ge(fills_made, 5)

            def inverse_root(k, p, moments_done):
                pool.wait_ge(ln_moments[k], moments_done)
                pool.tensor_tensor(var_eps[:, k], mean_var[:, k, :, 1], eps[:], ALU.add).then_inc(ln_eps[k], 1)
                pool.wait_ge(ln_eps[k], done(p))
                pool.tensor_tensor(rstd[:, k], var_eps[:, k], minus_half[:], ALU.pow).then_inc(ln_rstd[k], 1)

            def step(t, par, on):
                p0, p1, p2, p3, p4, p5 = [t - s for s in range(STREAMS)]
                entry, front, middle, relation, gat, last_layer = on

                if front:
                    pool.wait_ge(x_in[1 - par], 8 * (p1 - (1 - par) + 2))
                    pool.tensor_tensor(xb[:, 1 - par], x0[:, 1 - par], both(beta_ln_bc), ALU.add).then_inc(xb_ready, 1)
                if relation:
                    wait_before(pool, z_ready[1], p3)
                    inverse_root(1, p3, done(p3, 2))
                if last_layer:
                    pool.wait_ge(x3_ready, done(p5))
                    wait_before(pool, x4_ready, p5)
                    pool.tensor_tensor(x3b[:], x3[:, 1 - par], both(b_out_bc), ALU.add).then_inc(x3b_ready, 1)
                if relation:
                    pool.wait_ge(h1_full_ready, done(p3))
                    wait_before(pool, v1_psum, p3)
                    pool.tensor_tensor(h_t[1][1][:], h_t1_full[:], h_t[1][0][:].bitcast(f32), ALU.subtract)\
                        .then_inc(h_lo_ready[1], 1)
                if entry:
                    wait_before(pool, z_ready[0], p0)
                    inverse_root(0, p0, done(p0, 2))
                if gat:
                    pool.wait_ge(e_leaky_ready, done(p4))
                    pool.tensor_tensor(e_mask[:], e_leaky[:], both(adj_sb), ALU.mult).then_inc(e_mask_ready, 1)
                if relation:
                    pool.wait_ge(rel_ready, done(p3))
                    wait_before(pool, sum_sq_psum, p3)
                    pool.tensor_tensor(rel_sq[:], rel[:], rel[:], ALU.mult).then_inc(rel_sq_ready, 1)
                    pool.wait_ge(sum_sq_ready, done(p3))
                    wait_before(pool, x2_ready, p3, 2)
                    pool.tensor_tensor(inv_norm[:], sum_sq[:], minus_half[:], ALU.pow).then_inc(inv_norm_ready, 1)
                if gat:
                    wait_before(pool, h3_ready, p4)
                    inverse_root(3, p4, done(p4, 2))
                if middle:
                    wait_before(pool, x1_ready, p2, 2)
                    pool.wait_ge(o_ready, done(p2))
                    pool.wait_ge(xb_ready, done(p2))
                    pool.tensor_tensor(o_res[:], o[:], xb[:, par], ALU.add).then_inc(o_res_ready, 1)
                if relation:
                    wait_before(pool, z_ready[2], p3)
                    inverse_root(2, p3, done(p3, 2))
                if middle:
                    inverse_root(LN_O, p2, done(p2, 2))

            run(pool, step)


def kernel(**inputs):
    import concourse.bacc as bacc
    from concourse.bass_utils import run_bass_kernel_spmd

    def laid(a):
        return np.ascontiguousarray(np.asarray(a))

    arrays = {
        "x": laid(inputs["x"]),
        "adj": laid(inputs["adj"]),
        "adj_t": laid(np.asarray(inputs["adj"]).T),
        "w_qkv": laid(inputs["L0_gnn_w_qkv"]),
        "w_proj": laid(inputs["L0_gnn_w_proj"]),
        "b_proj": laid(inputs["L0_gnn_b_proj"]),
        "gamma": laid(inputs["L0_gnn_ln_gamma"]),
        "beta_ln": laid(inputs["L0_gnn_ln_beta"]),
        "w_q": laid(inputs["L1_gnn_Wq"]),
        "w_k": laid(inputs["L1_gnn_Wk"]),
        "w_v_t": laid(np.asarray(inputs["L1_gnn_Wv"]).T),
        "w_gat": laid(inputs["L2_gnn_W"]),
        "a_gat": laid(np.asarray(inputs["L2_gnn_a"]).reshape(2, -1)),
        "beta_gat": laid(inputs["L2_gnn_beta"]),
        "w_out": laid(inputs["L3_gnn_weight"]),
        "b_out": laid(inputs["L3_gnn_bias"]),
    }
    nc = bacc.Bacc("TRN2", target_bir_lowering=False, num_devices=1)
    args = [nc.dram_tensor(f"in_{k}", a.shape, mybir.dt.from_np(a.dtype), kind="ExternalInput").ap()
            for k, a in arrays.items()]
    out = nc.dram_tensor("out_x", arrays["x"].shape, mybir.dt.float32, kind="ExternalOutput").ap()
    order = ["x", "adj", "adj_t", "w_qkv", "w_proj", "b_proj", "gamma", "beta_ln", "w_q", "w_k", "w_v_t",
             "w_gat", "a_gat", "beta_gat", "w_out", "b_out"]
    at = dict(zip(arrays, args))
    gnn_stack(nc, *[at[k] for k in order], out)
    r = run_bass_kernel_spmd(nc, [{f"in_{k}": a for k, a in arrays.items()}], core_ids=[0])
    return r.results[0]["out_x"]
```

```python
import numpy as np
import concourse.bass as bass
from concourse import mybir
from contextlib import ExitStack


def gnn_stack(nc, x, adj, adj_t, w_qkv, w_proj, b_proj, gamma, beta_ln, w_q, w_k, w_v_t,
              w_gat, a_gat, beta_gat, w_out, b_out, out):
    f32 = mybir.dt.float32
    f32r = mybir.dt.float32r
    bf16 = mybir.dt.bfloat16
    ALU = mybir.AluOpType
    ACT = mybir.ActivationFunctionType
    AX = mybir.AxisListType

    B, N, D = x.shape
    H = 8
    HD = D // H
    C = D // 128
    PAIRS = B // 2
    RG = 128 // HD
    HC = H // RG
    W33 = HD + 1
    SCALE = float(HD) ** -0.5
    EPS = 1e-5
    MASKED = -1e30
    STREAMS = 6
    STEPS = 4
    FIRST = STREAMS + (PAIRS - STREAMS) % STEPS

    x_pairs = x.rearrange("(t b) n d -> t n b d", b=2)
    out_pairs = out.rearrange("(t b) n d -> t n b d", b=2)

    ctx = ExitStack()
    with ctx:
        def sb(name, shape, dt=f32):
            return ctx.enter_context(nc.sbuf_tensor(name, shape, dt))

        def sem(name):
            return ctx.enter_context(nc.semaphore(name))

        def parts(name, shape):
            return [sb(f"{name}_{part}", shape, f32r) for part in ("hi", "lo")]

        adj_sb = sb("adj_sb", [128, N])
        adj_t_sb = sb("adj_t_sb", [128, N])
        w_qkv_sb = sb("w_qkv_sb", [128, C, 3 * D])
        w_proj_sb = sb("w_proj_sb", [128, C, D])
        w_q_sb = sb("w_q_sb", [128, C, D])
        w_k_sb = sb("w_k_sb", [128, C, D])
        w_v_sb = sb("w_v_sb", [128, C, D])
        w_gat_sb = sb("w_gat_sb", [128, C, D])
        w_out_sb = sb("w_out_sb", [128, C, D])
        w_qk_sb = sb("w_qk_sb", [128, C, D])
        w_qkv_p = parts("w_qkv", [128, C, 3 * D])
        w_proj_p = parts("w_proj", [128, C, D])
        w_v_p = parts("w_v", [128, C, D])
        w_gat_p = parts("w_gat", [128, C, D])
        w_out_p = parts("w_out", [128, C, D])
        w_qk_p = parts("w_qk", [128, C, D])
        a_gat_bc = sb("a_gat_bc", [128, 2, D])
        b_proj_bc = sb("b_proj_bc", [128, D])
        gamma_bc = sb("gamma_bc", [128, D])
        beta_ln_bc = sb("beta_ln_bc", [128, D])
        b_out_bc = sb("b_out_bc", [128, D])
        beta_gat_bc = sb("beta_gat_bc", [128, 1])
        beta_ident = sb("beta_ident", [128, 128])
        b_out_less = sb("b_out_less", [128, D])
        ident = sb("ident", [128, 128])
        ident_b = sb("ident_b", [128, 128], bf16)
        mask_b = sb("mask_b", [128, N], bf16)
        ones = sb("ones", [128, 1])
        minus_half = sb("minus_half", [128, 2])
        eps = sb("eps", [128, 2])
        turn = sb("turn", [1, 1])

        x0 = sb("x0", [128, 2, 2, D])
        xb = sb("xb", [128, 2, 2, D])
        x1 = sb("x1", [128, 2, 2, D])
        x2 = sb("x2", [128, 2, 2, D])
        x3_up = sb("x3_up", [128, 2, 2, D])
        x3b = sb("x3b", [128, 2, D])
        x4 = sb("x4", [128, 2, 2, D])
        NORMS = 5
        LN_O = 4
        stats = sb("stats", [128, NORMS, 2, 6])
        mean_var = sb("mean_var", [128, NORMS, 2, 2])
        var_eps = sb("var_eps", [128, NORMS, 2])
        rstd = sb("rstd", [128, NORMS, 2])
        shift3 = sb("shift3", [128, 2])
        z = [sb(f"z{k}", [128, 2, D]) for k in range(3)]
        h_t = [parts(f"h_t{k}", [128, C, 2 * N]) for k in range(3)]
        h_t1_full = sb("h_t1_full", [128, C, 2 * N])
        q_t = sb("q_t", [128, 2, HC, 2 * N])
        k_diag = sb("k_diag", [128, HC, RG, 2 * N])
        v0 = sb("v0", [128, 2, 2, H, W33])
        BC = 2 * HC
        neg_max = sb("neg_max", [128, BC, RG])
        probs = sb("probs", [128, BC, RG, N])
        probs_t = sb("probs_t", [128, BC, RG, N])
        inv_sum = sb("inv_sum", [128, 2, H])
        o_heads = sb("o_heads", [128, 2, D])
        o_t = parts("o_t", [128, 2, C, N])
        o = sb("o", [128, 2, D])
        o_res = sb("o_res", [128, 2, D])
        o_gam = sb("o_gam", [128, 2, D])
        g_t = sb("g_t", [128, C, 2 * N])
        v1 = sb("v1", [128, 2, D])
        rel = sb("rel", [128, 2, N])
        rel_sq = sb("rel_sq", [128, 2, N])
        sum_sq = sb("sum_sq", [128, 2])
        inv_norm = sb("inv_norm", [128, 2])
        hw = sb("hw", [128, 2, D])
        s_prod = sb("s_prod", [128, 2, 2, D])
        s_sb = sb("s_sb", [128, 2, 2])
        e_sum = sb("e_sum", [128, 2, N])
        e_leaky = sb("e_leaky", [128, 2, N])
        e_mask = sb("e_mask", [128, 2, N])
        e_neg_max = sb("e_neg_max", [128, 2])
        att = sb("att", [128, 2, N])
        att_sum = sb("att_sum", [128, 2])
        att_inv = sb("att_inv", [128, 2])
        att_norm = sb("att_norm", [128, 2, N])
        att_t = sb("att_t", [128, 2, N])
        u_exp = sb("u_exp", [128, 2, D])
        x2_exp = sb("x2_exp", [128, 2, D])
        h3 = sb("h3", [128, 2, D])
        y_t = parts("y_t", [128, C, 2 * N])

        mid = ctx.enter_context(nc.psum_tensor("mid", [128, BC, 512], f32))
        bank4 = ctx.enter_context(nc.psum_tensor("bank4", [128, 512], f32))
        bank5 = ctx.enter_context(nc.psum_tensor("bank5", [128, 512], f32))
        bank6 = ctx.enter_context(nc.psum_tensor("bank6", [128, 512], f32))
        bank7 = ctx.enter_context(nc.psum_tensor("bank7", [128, 512], f32))

        w_qkv_in, fold_in, const_in = sem("w_qkv_in"), sem("fold_in"), sem("const_in")
        x_in = [sem(f"x_in{i}") for i in range(2)]
        x_out = [sem(f"x_out{i}") for i in range(2)]
        idents_zeroed, ident_made, fills_made = sem("idents_zeroed"), sem("ident_made"), sem("fills_made")
        mask_made, folded, folded_ready = sem("mask_made"), sem("folded"), sem("folded_ready")
        gat_consts_made = sem("gat_consts_made")
        w_hi_ready, w_lo_ready, split_ready = sem("w_hi_ready"), sem("w_lo_ready"), sem("split_ready")
        ln_stats = [sem(f"ln_stats{k}") for k in range(NORMS)]
        ln_moments = [sem(f"ln_moments{k}") for k in range(NORMS)]
        ln_eps = [sem(f"ln_eps{k}") for k in range(NORMS)]
        ln_rstd = [sem(f"ln_rstd{k}") for k in range(NORMS)]
        z_ready = [sem(f"z_ready{k}") for k in range(3)]
        h_t_psum = [sem(f"h_t_psum{k}") for k in range(3)]
        h_hi_ready = [sem(f"h_hi_ready{k}") for k in range(3)]
        h_lo_ready = [sem(f"h_lo_ready{k}") for k in range(3)]
        xb_ready, h1_full_ready = sem("xb_ready"), sem("h1_full_ready")
        q_psum, k_psum, v0_psum = sem("q_psum"), sem("k_psum"), sem("v0_psum")
        q_ready, k_ready, v0_ready = sem("q_ready"), [sem(f"k_ready{i}") for i in range(2)], sem("v0_ready")
        scores_psum, max_ready = sem("scores_psum"), sem("max_ready")
        probs_ready, probs_t_psum, probs_t_ready = sem("probs_ready"), sem("probs_t_psum"), sem("probs_t_ready")
        heads_psum, inv_sum_ready, o_heads_ready = sem("heads_psum"), sem("inv_sum_ready"), sem("o_heads_ready")
        o_t_psum, o_hi_ready, o_lo_ready = sem("o_t_psum"), sem("o_hi_ready"), sem("o_lo_ready")
        o_psum, o_ready = sem("o_psum"), sem("o_ready")
        o_res_ready, o_gam_ready, x1_ready = sem("o_res_ready"), sem("o_gam_ready"), sem("x1_ready")
        g_psum, g_ready, v1_psum, v1_ready = sem("g_psum"), sem("g_ready"), sem("v1_psum"), sem("v1_ready")
        rel_psum, rel_ready, rel_sq_ready = sem("rel_psum"), sem("rel_ready"), sem("rel_sq_ready")
        sum_sq_psum, sum_sq_ready, inv_norm_ready = sem("sum_sq_psum"), sem("sum_sq_ready"), sem("inv_norm_ready")
        rel_v_psum, x2_ready = sem("rel_v_psum"), sem("x2_ready")
        hw_psum, hw_ready, s_ready = sem("hw_psum"), sem("hw_ready"), sem("s_ready")
        s2_psum, e_sum_ready, e_leaky_ready, e_mask_ready, e_max_ready = (
            sem("s2_psum"), sem("e_sum_ready"), sem("e_leaky_ready"), sem("e_mask_ready"), sem("e_max_ready"))
        att_ready, att_inv_ready, att_norm_ready, att_t_psum, att_t_ready = (
            sem("att_ready"), sem("att_inv_ready"), sem("att_norm_ready"), sem("att_t_psum"), sem("att_t_ready"))
        u_psum, u_exp_ready, x2_exp_ready, x3_ready, x3b_ready = (
            sem("u_psum"), sem("u_exp_ready"), sem("x2_exp_ready"), sem("x3_ready"), sem("x3b_ready"))
        shift3_ready, h3_ready, y_t_psum, y_hi_ready, y_lo_ready, y_psum, x4_ready = (
            sem("shift3_ready"), sem("h3_ready"), sem("y_t_psum"), sem("y_hi_ready"), sem("y_lo_ready"),
            sem("y_psum"), sem("x4_ready"))

        block = ctx.enter_context(nc.Block())

        def done(p, n=1):
            return (p + 1) * n

        def wait_before(eng, s, p, n=1):
            if not isinstance(p, int) or p > 0:
                eng.wait_ge(s, p * n)

        def streams(t):
            return [0 <= t - s < PAIRS for s in range(STREAMS)]

        def run(eng, step, set_up):
            for t in range(FIRST):
                step(t, t % 2, streams(t))
                if t in set_up:
                    set_up[t]()
            with eng.Fori(FIRST, PAIRS - STEPS + 1, STEPS) as t:
                for i in range(STEPS):
                    step(t + i if i else t, i % 2, [True] * STREAMS)
            for t in range(PAIRS, PAIRS + STREAMS - 1):
                step(t, t % 2, streams(t))

        def both(row):
            return row[:].unsqueeze(1).to_broadcast([128, 2, row.shape[-1]])

        FIRST_CONSTS = [
            (w_qkv_sb, w_qkv.rearrange("(c p) n -> p c n", p=128), w_qkv_in),
            (w_q_sb, w_q.rearrange("(c p) n -> p c n", p=128), fold_in),
            (w_k_sb, w_k.rearrange("(c p) n -> p c n", p=128), fold_in),
        ]
        CONSTS = [
            (adj_sb, adj),
            (adj_t_sb, adj_t),
            (w_proj_sb, w_proj.rearrange("(c p) n -> p c n", p=128)),
            (w_v_sb, w_v_t.rearrange("(c p) n -> p c n", p=128)),
            (w_gat_sb, w_gat.rearrange("(c p) n -> p c n", p=128)),
            (w_out_sb, w_out.rearrange("(c p) n -> p c n", p=128)),
            (b_proj_bc, b_proj.partition_broadcast(128)),
            (gamma_bc, gamma.partition_broadcast(128)),
            (beta_ln_bc, beta_ln.partition_broadcast(128)),
            (b_out_bc, b_out.partition_broadcast(128)),
            (a_gat_bc, a_gat.partition_broadcast(128)),
            (beta_gat_bc, beta_gat.partition_broadcast(128)),
        ]
        ALL_CONSTS = 16 * len(CONSTS)
        SPLIT = [(w_proj_sb, w_proj_p), (w_v_sb, w_v_p), (w_gat_sb, w_gat_p), (w_out_sb, w_out_p)]

        def keys_apart(eng, p, half):
            eng.wait_ge(k_psum, done(p))
            for r in range(half * RG // 2, (half + 1) * RG // 2):
                at = slice(r * HD, (r + 1) * HD)
                dst, src = k_diag[at, :, r, :], bank6[at, :].rearrange("p (h n) -> p h n", h=HC)
                last = eng.tensor_copy(dst, src) if half else eng.activation(dst, src, ACT.Copy)
            last.then_inc(k_ready[half], 1)

        @block.sync
        def _(sp):
            sp.dma_start(x0[:, 0], x_pairs[0]).then_inc(x_in[0], 16)
            for dst, src, signal in FIRST_CONSTS:
                sp.dma_start(dst[:], src).then_inc(signal, 16)
            sp.dma_start(x0[:, 1], x_pairs[1]).then_inc(x_in[1], 16)
            for dst, src in CONSTS:
                sp.dma_start(dst[:], src).then_inc(const_in, 16)

            def step(t, par, load, store):
                p1, p5 = t - 1, t - 5
                peeled = isinstance(t, int)
                if load:
                    sp.wait_ge(z_ready[0], done(p1))
                    sp.wait_ge(xb_ready, done(p1))
                    sp.dma_start(x0[:, 1 - par], x_pairs[p1 + 2] if peeled else x_pairs[bass.ds(p1 + 2, 1)][0])\
                      .then_inc(x_in[1 - par], 16)
                if store:
                    sp.wait_ge(x4_ready, done(p5))
                    sp.dma_start(out_pairs[p5] if peeled else out_pairs[bass.ds(p5, 1)][0],
                                 x4[:, 1 - par]).then_inc(x_out[1 - par], 16)

            for t in range(STREAMS):
                step(t, t % 2, t >= 1, t >= 5)
            with sp.Fori(STREAMS, PAIRS - 3, 2) as t:
                step(t, 0, True, True)
                step(t + 1, 1, True, True)
            for t in range(PAIRS - 2, PAIRS + STREAMS - 1):
                step(t, t % 2, t == PAIRS - 2, True)
            for i in range(2):
                sp.wait_ge(x_out[i], 16 * (PAIRS // 2))

        @block.tensor
        def _(pe):
            def product(dst, lhs_t, rhs, pick_l, pick_r):
                terms = [(c, a, b) for c in range(C) for a, b in ((0, 0), (0, 1), (1, 0))]
                for n, (c, a, b) in enumerate(terms):
                    last = pe.matmul(dst, pick_l(lhs_t[a], c), pick_r(rhs[b], c),
                                     start=n == 0, stop=n == len(terms) - 1)
                return last

            def transposes(dst, src, k):
                for b in range(2):
                    for c in range(C):
                        last = pe.transpose(dst[:, (c * 2 + b) * N:(c * 2 + b + 1) * N],
                                            src[:, b, c * 128:(c + 1) * 128], ident[:])
                last.then_inc(h_t_psum[k], 1)

            def rows(dst, h, w, w0, signal):
                for b in range(2):
                    last = product(dst[:, b * D:(b + 1) * D], h, w,
                                   lambda a, c: a[:, c, b * N:(b + 1) * N], lambda a, c: a[:, c, w0:w0 + D])
                last.then_inc(signal, 1)

            def columns(dst, w, w0, h, signal):
                for j in range(C):
                    last = product(dst[:, j * 2 * N:(j + 1) * 2 * N], w, h,
                                   lambda a, c: a[:, c, w0 + j * 128:w0 + (j + 1) * 128], lambda a, c: a[:, c])
                last.then_inc(signal, 1)

            pe.wait_ge(ident_made, 2)

            def fold():
                pe.wait_ge(fold_in, 16 * 2)
                for j in range(C):
                    for c in range(C):
                        last = pe.matmul(bank4[:, j * D:(j + 1) * D], w_q_sb[:, c, j * 128:(j + 1) * 128],
                                         w_k_sb[:, c, :], start=c == 0, stop=c == C - 1)
                last.then_inc(folded, 1)
                pe.wait_ge(w_hi_ready, 1)
                pe.wait_ge(w_lo_ready, 1)

            def masks_and_fills():
                pe.wait_ge(fills_made, 5)
                pe.wait_ge(mask_made, 1)

            def other_weights():
                pe.wait_ge(split_ready, 2 * len(SPLIT))
                pe.wait_ge(w_lo_ready, 2)

            def step(t, par, on):
                p0, p1, p2, p3, p4, p5 = [t - s for s in range(STREAMS)]
                entry, front, middle, relation, gat, last_layer = on
                peeled = isinstance(t, int)
                on_before = streams(t - 1) if peeled else on

                def transpose_probs(s):
                    pe.wait_ge(probs_ready, done(p2, BC) - (BC - 1 - s))
                    for r in range(RG):
                        last = pe.transpose(mid[:, s, r * N:(r + 1) * N], probs[:, s, r], ident[:])
                    last.then_inc(probs_t_psum, 1)

                def scores(b):
                    for hc in range(HC):
                        s = b * HC + hc
                        pe.matmul(mid[:, s], ident_b[:], mask_b[:].unsqueeze(1).to_broadcast([128, RG, N]),
                                  start=True, stop=False)
                        last = pe.matmul(mid[:, s], q_t[:, par, hc, b * N:(b + 1) * N],
                                         k_diag[:, hc, :, b * N:(b + 1) * N], start=False, stop=True)
                    last.then_inc(scores_psum, 1)

                def heads_times_values(b):
                    pe.wait_ge(probs_t_ready, done(p2, BC) - HC * (1 - b))
                    for h in range(H):
                        last = pe.matmul(mid[:, b, h * W33:(h + 1) * W33], probs_t[:, b * HC + h // RG, h % RG],
                                         v0[:, par, b, h], start=True, stop=True)
                    last.then_inc(heads_psum, 1)

                if middle:
                    pe.wait_ge(q_ready, done(p2))
                    pe.wait_ge(k_ready[0], done(p2))
                    pe.wait_ge(k_ready[1], done(p2))
                    wait_before(pe, o_heads_ready, p2, 2)
                    scores(0)
                if front:
                    pe.wait_ge(h_hi_ready[0], done(p1))
                    pe.wait_ge(h_lo_ready[0], done(p1))
                    if on_before[3]:
                        wait_before(pe, x2_ready, p3, 2)
                    elif on_before[1]:
                        wait_before(pe, k_ready[0], p1)
                        wait_before(pe, k_ready[1], p1)
                    columns(bank6, w_qkv_p, 0, h_t[0], q_psum)
                if relation:
                    pe.wait_ge(o_hi_ready, done(p3))
                    pe.wait_ge(o_lo_ready, done(p3))
                    for b in range(2):
                        last = product(mid[:, 3, b * D:(b + 1) * D], o_t, w_proj_p,
                                       lambda a, c: a[:, b, c], lambda a, c: a[:, c])
                    last.then_inc(o_psum, 1)
                if front:
                    pe.wait_ge(q_ready, done(p1))
                    rows(bank6, h_t[0], w_qkv_p, 2 * D, v0_psum)
                if middle:
                    wait_before(pe, o_lo_ready, p2)
                    wait_before(pe, o_ready, p2)
                    scores(1)
                if gat:
                    pe.wait_ge(z_ready[2], done(p4))
                    wait_before(pe, x3_ready, p4)
                    transposes(bank4, z[2], 2)
                if middle:
                    transpose_probs(0)
                if last_layer:
                    pe.wait_ge(h3_ready, done(p5))
                    if on_before[0]:
                        pe.wait_ge(h_lo_ready[0], done(p1))
                    elif on_before[3]:
                        wait_before(pe, v1_ready, p3)
                    else:
                        wait_before(pe, x4_ready, p5)
                    for c in range(C):
                        for b in range(2):
                            last = pe.matmul(bank7[:, (c * 2 + b) * N:(c * 2 + b + 1) * N],
                                             h3[:, b, c * 128:(c + 1) * 128], adj_t_sb[:], start=True, stop=True)
                    last.then_inc(y_t_psum, 1)
                if middle:
                    transpose_probs(1)
                if gat:
                    pe.wait_ge(h_hi_ready[2], done(p4))
                    pe.wait_ge(h_lo_ready[2], done(p4))
                    rows(bank4, h_t[2], w_gat_p, 0, hw_psum)
                if front:
                    pe.wait_ge(v0_ready, done(p1))
                    columns(bank6, w_qkv_p, D, h_t[0], k_psum)
                if relation:
                    pe.wait_ge(z_ready[1], done(p3))
                    wait_before(pe, sum_sq_ready, p3)
                    transposes(bank5, z[1], 1)
                if last_layer:
                    pe.wait_ge(y_hi_ready, done(p5))
                    pe.wait_ge(y_lo_ready, done(p5))
                    rows(bank7, y_t, w_out_p, 0, y_psum)
                if middle:
                    transpose_probs(2)
                if middle:
                    transpose_probs(3)
                if gat:
                    pe.wait_ge(s_ready, done(p4, 4))
                    pe.wait_ge(hw_ready, done(p4))
                    for b in range(2):
                        last = pe.transpose(bank4[:, 256 + b * N:256 + (b + 1) * N],
                                            s_sb[:, b, 1:2].to_broadcast([128, 128]), ident[:])
                    last.then_inc(s2_psum, 1)
                if relation:
                    pe.wait_ge(h_hi_ready[1], done(p3))
                    pe.wait_ge(h_lo_ready[1], done(p3))
                    pe.wait_ge(h1_full_ready, done(p3))
                    columns(bank5, w_qk_p, 0, h_t[1], g_psum)
                if relation:
                    if last_layer:
                        pe.wait_ge(x4_ready, done(p5))
                    elif entry or on_before[0]:
                        pe.wait_ge(h_lo_ready[0], done(p1))
                    rows(bank7, h_t[1], w_v_p, 0, v1_psum)
                if relation:
                    pe.wait_ge(g_ready, done(p3))
                    for b in range(2):
                        for c in range(C):
                            last = pe.matmul(bank5[:, b * N:(b + 1) * N], h_t1_full[:, c, b * N:(b + 1) * N],
                                             g_t[:, c, b * N:(b + 1) * N], start=c == 0, stop=c == C - 1)
                    last.then_inc(rel_psum, 1)
                if middle:
                    heads_times_values(0)
                if gat:
                    pe.wait_ge(att_norm_ready, done(p4, 2))
                    for b in range(2):
                        last = pe.transpose(bank4[:, b * N:(b + 1) * N], att_norm[:, b], ident[:])
                    last.then_inc(att_t_psum, 1)
                if relation:
                    if front:
                        pe.wait_ge(k_ready[0], done(p1))
                        pe.wait_ge(k_ready[1], done(p1))
                    elif on_before[3]:
                        wait_before(pe, x2_ready, p3, 2)
                    pe.wait_ge(v1_ready, done(p3))
                    pe.wait_ge(rel_ready, done(p3))
                    for b in range(2):
                        last = pe.matmul(bank6[:, b * D:(b + 1) * D], rel[:, b], v1[:, b], start=True, stop=True)
                    last.then_inc(rel_v_psum, 1)
                if gat:
                    pe.wait_ge(att_t_ready, done(p4))
                    for b in range(2):
                        last = pe.matmul(bank4[:, b * D:(b + 1) * D], att_t[:, b], hw[:, b], start=True, stop=True)
                    last.then_inc(u_psum, 1)
                if middle:
                    heads_times_values(1)
                if relation:
                    pe.wait_ge(rel_sq_ready, done(p3))
                    for b in range(2):
                        last = pe.matmul(bank5[:, 256 + b:257 + b], rel_sq[:, b], ones[:], start=True, stop=True)
                    last.then_inc(sum_sq_psum, 1)
                if entry:
                    pe.wait_ge(z_ready[0], done(p0))
                    if relation:
                        pe.wait_ge(v1_ready, done(p3))
                    elif on_before[0]:
                        wait_before(pe, h_lo_ready[0], p0)
                    transposes(bank7, z[0], 0)
                if middle:
                    for b in range(2):
                        pe.wait_ge(o_heads_ready, done(p2, 2) - (1 - b))
                        for c in range(C):
                            last = pe.transpose(mid[:, 2, (b * C + c) * N:(b * C + c + 1) * N],
                                                o_heads[:, b, c * 128:(c + 1) * 128], ident[:])
                    last.then_inc(o_t_psum, 1)

            run(pe, step, {0: fold, 1: masks_and_fills, 2: other_weights})

        @block.scalar
        def _(act):
            act.wait_ge(w_qkv_in, 16)
            act.activation(w_qkv_p[0][:], w_qkv_sb[:], ACT.Copy).then_inc(w_hi_ready, 1)

            def copy_fold():
                act.wait_ge(folded, 1)
                act.activation(w_qk_sb[:], bank4[:], ACT.Copy).then_inc(folded_ready, 1)
                act.activation(w_qk_p[0][:], bank4[:], ACT.Copy).then_inc(w_hi_ready, 1)
                act.wait_ge(const_in, ALL_CONSTS)

            def step(t, par, on):
                p0, p1, p2, p3, p4, p5 = [t - s for s in range(STREAMS)]
                entry, front, middle, relation, gat, last_layer = on

                def relu_hi(k, p, bank, users):
                    act.wait_ge(h_t_psum[k], done(p))
                    for psum in users:
                        wait_before(act, psum, p)
                    act.activation(h_t[k][0][:], bank[:], ACT.Relu).then_inc(h_hi_ready[k], 1)

                def exps(s):
                    if s % 2 == 0:
                        act.wait_ge(max_ready, done(p2, 2) - (1 - s // 2))
                    wait_before(act, probs_t_psum, p2, BC)
                    for r in range(RG):
                        last = act.activation(probs[:, s, r], mid[:, s, r * N:(r + 1) * N], ACT.Exp,
                                              bias=neg_max[:, s, r:r + 1])
                    last.then_inc(probs_ready, 1)

                def copy_probs_t(s):
                    act.wait_ge(probs_t_psum, done(p2, BC) - (BC - 1 - s))
                    wait_before(act, heads_psum, p2, 2)
                    act.activation(probs_t[:, s], mid[:, s], ACT.Copy).then_inc(probs_t_ready, 1)

                if front:
                    act.wait_ge(q_psum, done(p1))
                    act.activation(q_t[:, 1 - par], bank6[:], ACT.Copy, scale=SCALE).then_inc(q_ready, 1)
                if middle:
                    exps(0)
                if middle:
                    exps(1)
                if last_layer:
                    act.wait_ge(shift3_ready, done(p5))
                    wait_before(act, y_t_psum, p5)
                    for b in range(2):
                        last = act.activation(h3[:, b], x3_up[:, 1 - par, b], ACT.Relu, bias=shift3[:, b:b + 1],
                                              scale=rstd[:, 3, b:b + 1])
                    last.then_inc(h3_ready, 1)
                if gat:
                    relu_hi(2, p4, bank4, [hw_psum])
                if front:
                    act.wait_ge(v0_psum, done(p1))
                    act.activation(v0[:, 1 - par, :, :, 0:HD], bank6[:].rearrange("p (b h d) -> p b h d", b=2, h=H),
                                   ACT.Copy).then_inc(v0_ready, 1)
                if last_layer:
                    act.wait_ge(y_t_psum, done(p5))
                    wait_before(act, y_psum, p5)
                    act.activation(y_t[0][:], bank7[:], ACT.Copy).then_inc(y_hi_ready, 1)
                if middle:
                    copy_probs_t(0)
                if middle:
                    copy_probs_t(1)
                if gat:
                    act.wait_ge(hw_psum, done(p4))
                    act.activation(hw[:], bank4[:], ACT.Copy).then_inc(hw_ready, 1)
                if middle:
                    exps(2)
                if relation:
                    relu_hi(1, p3, bank5, [v1_psum])
                if middle:
                    exps(3)
                if relation:
                    act.wait_ge(h_lo_ready[1], done(p3))
                    wait_before(act, rel_psum, p3)
                    act.activation(h_t1_full[:], bank5[:], ACT.Relu).then_inc(h1_full_ready, 1)
                if gat:
                    act.wait_ge(s2_psum, done(p4))
                    for b in range(2):
                        act.activation(e_sum[:, b], bank4[:, 256 + b * N:256 + (b + 1) * N], ACT.Identity,
                                       bias=s_sb[:, b, 0:1]).then_inc(e_sum_ready, 1)
                if middle:
                    copy_probs_t(2)
                if middle:
                    copy_probs_t(3)
                if relation:
                    act.wait_ge(g_psum, done(p3))
                    act.activation(g_t[:], bank5[:], ACT.Copy).then_inc(g_ready, 1)
                if front:
                    keys_apart(act, p1, 0)
                if gat:
                    act.wait_ge(e_max_ready, done(p4))
                    wait_before(act, att_norm_ready, p4, 2)
                    for b in range(2):
                        act.activation(att[:, b], e_mask[:, b], ACT.Exp, bias=e_neg_max[:, b:b + 1],
                                       accum_out=att_sum[:, b:b + 1]).then_inc(att_ready, 1)
                if relation:
                    act.wait_ge(v1_psum, done(p3))
                    act.activation(v1[:], bank7[:], ACT.Copy).then_inc(v1_ready, 1)
                if gat:
                    act.wait_ge(att_t_psum, done(p4))
                    act.activation(att_t[:], bank4[:, 0:2 * N], ACT.Copy).then_inc(att_t_ready, 1)
                if gat:
                    act.wait_ge(u_psum, done(p4))
                    wait_before(act, x2_exp_ready, p4)
                    act.activation(u_exp[:].rearrange("p b d -> p (b d)"), bank4[:], ACT.Exp).then_inc(u_exp_ready, 1)
                if entry:
                    relu_hi(0, p0, bank7, [k_psum])
                if middle:
                    act.wait_ge(o_t_psum, done(p2))
                    act.activation(o_t[0][:], mid[:, 2], ACT.Copy).then_inc(o_hi_ready, 1)

            run(act, step, {1: copy_fold})

        @block.vector
        def _(dve):
            def split_w_qkv():
                dve.wait_ge(w_hi_ready, 1)
                dve.tensor_tensor(w_qkv_p[1][:], w_qkv_sb[:], w_qkv_p[0][:].bitcast(f32), ALU.subtract)\
                   .then_inc(w_lo_ready, 1)

            def derive_constants():
                dve.wait_ge(const_in, ALL_CONSTS)
                dve.tensor_scalar(mask_b[:], adj_sb[:], 0.0, MASKED, ALU.is_equal, ALU.mult).then_inc(mask_made, 1)
                dve.wait_ge(ident_made, 2)
                dve.tensor_scalar(beta_ident[:], ident[:], beta_gat_bc[:], None, ALU.mult).then_inc(gat_consts_made, 1)
                dve.tensor_scalar(b_out_less[:], b_out_bc[:], -1.0, None, ALU.add).then_inc(gat_consts_made, 1)
                dve.wait_ge(gat_consts_made, 2)

            def split_w_qk():
                dve.wait_ge(folded_ready, 1)
                dve.wait_ge(w_hi_ready, 2)
                dve.tensor_tensor(w_qk_p[1][:], w_qk_sb[:], w_qk_p[0][:].bitcast(f32), ALU.subtract)\
                   .then_inc(w_lo_ready, 1)

            def moments(k, p, src):
                wait_before(dve, ln_rstd[k], p)
                for b in range(2):
                    dve.bn_stats(stats[:, k, b], src[:, b]).then_inc(ln_stats[k], 1)
                dve.wait_ge(ln_stats[k], done(p, 2))
                dve.memset(turn[:], 0.0)
                for b in range(2):
                    dve.bn_aggr(mean_var[:, k, b], stats[:, k, b]).then_inc(ln_moments[k], 1)

            def normalize(k, p, dst, src, signal):
                dve.wait_ge(ln_rstd[k], done(p))
                for b in range(2):
                    last = dve.tensor_scalar(dst[:, b], src[:, b], mean_var[:, k, b, 0:1], rstd[:, k, b:b + 1],
                                             ALU.subtract, ALU.mult)
                last.then_inc(signal, 1)

            def relu_lo(k, p, bank):
                dve.wait_ge(h_hi_ready[k], done(p))
                dve.scalar_tensor_tensor(h_t[k][1][:].rearrange("p c n -> p (c n)"), bank[:], 0.0,
                                         h_t[k][0][:].rearrange("p c n -> p (c n)").bitcast(f32),
                                         ALU.max, ALU.subtract).then_inc(h_lo_ready[k], 1)

            def step(t, par, on):
                p0, p1, p2, p3, p4, p5 = [t - s for s in range(STREAMS)]
                entry, front, middle, relation, gat, last_layer = on

                def maxima(half):
                    dve.wait_ge(scores_psum, done(p2, 2) - (1 - half))
                    if half == 0:
                        wait_before(dve, probs_ready, p2, BC)
                    at = slice(2 * half, 2 * half + 2)
                    dve.tensor_reduce(neg_max[:, at], mid[:, at].rearrange("p s (r m) -> p s r m", m=N),
                                      op=ALU.max, axis=AX.X, negate=True).then_inc(max_ready, 1)

                def projections_on_a(b):
                    for j in range(2):
                        dve.tensor_tensor_reduce(out=s_prod[:, b, j], in0=hw[:, b], in1=a_gat_bc[:, j],
                                                 scale=1.0, scalar=0.0, op0=ALU.mult, op1=ALU.add,
                                                 accum_out=s_sb[:, b, j:j + 1]).then_inc(s_ready, 1)

                def divide_heads(b):
                    heads = mid[:, b, 0:H * W33].rearrange("p (h d) -> p h d", h=H)
                    dve.wait_ge(heads_psum, done(p2, 2) - (1 - b))
                    dve.reciprocal(inv_sum[:, b], heads[:, :, HD]).then_inc(inv_sum_ready, 1)
                    dve.wait_ge(inv_sum_ready, done(p2, 2) - (1 - b))
                    wait_before(dve, o_t_psum, p2)
                    dve.tensor_tensor(o_heads[:, b].rearrange("p (h d) -> p h d", h=H), heads[:, :, 0:HD],
                                      inv_sum[:, b].unsqueeze(2).to_broadcast([128, H, HD]), ALU.mult)\
                       .then_inc(o_heads_ready, 1)

                if middle:
                    maxima(0)
                if relation:
                    dve.wait_ge(o_psum, done(p3))
                    wait_before(dve, o_res_ready, p3)
                    dve.tensor_tensor(o[:], mid[:, 3].rearrange("p (b d) -> p b d", b=2), both(b_proj_bc), ALU.add)\
                       .then_inc(o_ready, 1)
                if last_layer:
                    dve.wait_ge(ln_rstd[3], done(p5))
                    wait_before(dve, h3_ready, p5)
                    dve.scalar_tensor_tensor(shift3[:], mean_var[:, 3, :, 0], -1.0, rstd[:, 3], ALU.mult, ALU.mult)\
                       .then_inc(shift3_ready, 1)
                if relation:
                    dve.wait_ge(o_ready, done(p3))
                    moments(LN_O, p3, o)
                if gat:
                    wait_before(dve, h_t_psum[2], p4)
                    normalize(2, p4, z[2], x2[:, par], z_ready[2])
                if relation:
                    dve.wait_ge(ln_moments[LN_O], done(p3, 2))
                    for b in range(2):
                        last = dve.scalar_tensor_tensor(o_gam[:, b], o[:, b], mean_var[:, LN_O, b, 0:1], gamma_bc[:],
                                                        ALU.subtract, ALU.mult)
                    last.then_inc(o_gam_ready, 1)
                if relation:
                    dve.wait_ge(o_gam_ready, done(p3))
                    dve.wait_ge(ln_rstd[LN_O], done(p3))
                    dve.wait_ge(o_res_ready, done(p3))
                    for b in range(2):
                        dve.scalar_tensor_tensor(x1[:, 1 - par, b], o_gam[:, b], rstd[:, LN_O, b:b + 1], o_res[:, b],
                                                 ALU.mult, ALU.add).then_inc(x1_ready, 1)
                if gat:
                    relu_lo(2, p4, bank4)
                if relation:
                    dve.wait_ge(x1_ready, done(p3, 2))
                    moments(1, p3, x1[:, 1 - par])
                if middle:
                    maxima(1)
                if relation:
                    wait_before(dve, h_t_psum[1], p3)
                    normalize(1, p3, z[1], x1[:, 1 - par], z_ready[1])
                if last_layer:
                    dve.wait_ge(y_hi_ready, done(p5))
                    dve.tensor_tensor(y_t[1][:].rearrange("p c n -> p (c n)"), bank7[:],
                                      y_t[0][:].rearrange("p c n -> p (c n)").bitcast(f32), ALU.subtract)\
                       .then_inc(y_lo_ready, 1)
                if gat:
                    dve.wait_ge(hw_ready, done(p4))
                    wait_before(dve, s2_psum, p4)
                    projections_on_a(0)
                if relation:
                    wait_before(dve, v1_psum, p3)
                    relu_lo(1, p3, bank5)
                if gat:
                    projections_on_a(1)
                if last_layer:
                    dve.wait_ge(y_psum, done(p5))
                    dve.wait_ge(x3b_ready, done(p5))
                    if not isinstance(t, int) or p5 > 1:
                        dve.wait_ge(x_out[1 - par], 8 * (p5 - (1 - par)))
                    dve.tensor_tensor(x4[:, 1 - par], bank7[:].rearrange("p (b d) -> p b d", b=2), x3b[:], ALU.add)\
                       .then_inc(x4_ready, 1)
                if entry:
                    dve.wait_ge(x_in[par], 8 * (p0 - par + 2))
                    moments(0, p0, x0[:, par])
                if gat:
                    dve.wait_ge(e_sum_ready, done(p4, 2))
                    dve.scalar_tensor_tensor(e_leaky[:], e_sum[:], 0.2, e_sum[:], ALU.mult, ALU.max)\
                       .then_inc(e_leaky_ready, 1)
                if front:
                    keys_apart(dve, p1, 1)
                if gat:
                    dve.wait_ge(e_mask_ready, done(p4))
                    wait_before(dve, att_ready, p4, 2)
                    dve.tensor_reduce(e_neg_max[:], e_mask[:], op=ALU.max, axis=AX.X, negate=True)\
                       .then_inc(e_max_ready, 1)
                if entry:
                    wait_before(dve, h_t_psum[0], p0)
                    normalize(0, p0, z[0], x0[:, par], z_ready[0])
                if gat:
                    dve.wait_ge(att_ready, done(p4, 2))
                    dve.reciprocal(att_inv[:], att_sum[:]).then_inc(att_inv_ready, 1)
                    dve.wait_ge(att_inv_ready, done(p4))
                    wait_before(dve, att_t_psum, p4)
                    for b in range(2):
                        dve.scalar_tensor_tensor(att_norm[:, b], att[:, b], att_inv[:, b:b + 1], beta_ident[:],
                                                 ALU.mult, ALU.add).then_inc(att_norm_ready, 1)
                if relation:
                    dve.wait_ge(rel_psum, done(p3))
                    wait_before(dve, rel_v_psum, p3)
                    dve.tensor_tensor(rel[:], bank5[:, 0:2 * N].rearrange("p (b n) -> p b n", b=2),
                                      both(adj_sb), ALU.mult).then_inc(rel_ready, 1)
                if middle:
                    divide_heads(0)
                if gat:
                    dve.wait_ge(u_exp_ready, done(p4))
                    dve.scalar_tensor_tensor(x2_exp[:], u_exp[:], 1.0, x2[:, par], ALU.min, ALU.add)\
                       .then_inc(x2_exp_ready, 1)
                    dve.wait_ge(x2_exp_ready, done(p4))
                    dve.scalar_tensor_tensor(x3_up[:, par], bank4[:].rearrange("p (b d) -> p b d", b=2), 0.0, x2_exp[:],
                                             ALU.max, ALU.add).then_inc(x3_ready, 1)
                if middle:
                    divide_heads(1)
                if relation:
                    dve.wait_ge(sum_sq_psum, done(p3))
                    dve.tensor_copy(sum_sq[:], bank5[:, 256:258]).then_inc(sum_sq_ready, 1)
                if entry:
                    relu_lo(0, p0, bank7)
                if relation:
                    dve.wait_ge(rel_v_psum, done(p3))
                    dve.wait_ge(inv_norm_ready, done(p3))
                    for b in range(2):
                        dve.scalar_tensor_tensor(x2[:, 1 - par, b], bank6[:, b * D:(b + 1) * D], inv_norm[:, b:b + 1],
                                                 x1[:, 1 - par, b], ALU.mult, ALU.add).then_inc(x2_ready, 1)
                if middle:
                    dve.wait_ge(o_hi_ready, done(p2))
                    wait_before(dve, o_psum, p2)
                    dve.tensor_tensor(o_t[1][:].rearrange("p b c n -> p (b c n)"), mid[:, 2],
                                      o_t[0][:].rearrange("p b c n -> p (b c n)").bitcast(f32), ALU.subtract)\
                       .then_inc(o_lo_ready, 1)
                if gat:
                    dve.wait_ge(x3_ready, done(p4))
                    moments(3, p4, x3_up[:, par])
                if relation:
                    dve.wait_ge(x2_ready, done(p3, 2))
                    moments(2, p3, x2[:, 1 - par])

            run(dve, step, {0: split_w_qkv, 1: derive_constants, 2: split_w_qk})

        @block.gpsimd
        def _(pool):
            for m in (ident, ident_b):
                pool.memset(m[:], 0.0).then_inc(idents_zeroed, 1)
            pool.memset(ones[:], 1.0).then_inc(fills_made, 1)
            pool.memset(minus_half[:], -0.5).then_inc(fills_made, 1)
            pool.memset(eps[:], EPS).then_inc(fills_made, 1)
            pool.memset(v0[:, :, :, :, HD:W33], 1.0).then_inc(fills_made, 1)
            pool.memset(k_diag[:], 0.0).then_inc(fills_made, 1)
            pool.wait_ge(idents_zeroed, 2)
            for m in (ident, ident_b):
                pool.affine_select(out=m[:], in_=m[:], compare_op=ALU.not_equal, fill=1.0, base=0,
                                   pattern=[[-1, 128]], channel_multiplier=1).then_inc(ident_made, 1)
            pool.wait_ge(fills_made, 5)

            def wait_for_constants():
                pool.wait_ge(const_in, ALL_CONSTS)

            def split_weights():
                pool.wait_ge(gat_consts_made, 2)
                for w, (hi, _) in SPLIT:
                    pool.tensor_copy(hi[:], w[:]).then_inc(split_ready, 1)
                pool.wait_ge(split_ready, len(SPLIT))
                for w, (hi, lo) in SPLIT:
                    pool.tensor_tensor(lo[:], w[:], hi[:].bitcast(f32), ALU.subtract).then_inc(split_ready, 1)

            def inverse_root(k, p, moments_done):
                pool.wait_ge(ln_moments[k], moments_done)
                pool.tensor_tensor(var_eps[:, k], mean_var[:, k, :, 1], eps[:], ALU.add).then_inc(ln_eps[k], 1)
                pool.wait_ge(ln_eps[k], done(p))
                pool.tensor_tensor(rstd[:, k], var_eps[:, k], minus_half[:], ALU.pow).then_inc(ln_rstd[k], 1)

            def step(t, par, on):
                p0, p1, p2, p3, p4, p5 = [t - s for s in range(STREAMS)]
                entry, front, middle, relation, gat, last_layer = on

                if relation:
                    wait_before(pool, x1_ready, p3, 2)
                    pool.wait_ge(o_ready, done(p3))
                    pool.wait_ge(xb_ready, done(p3))
                    pool.tensor_tensor(o_res[:], o[:], xb[:, 1 - par], ALU.add).then_inc(o_res_ready, 1)
                if relation:
                    inverse_root(LN_O, p3, done(p3, 2))
                if front:
                    pool.wait_ge(x_in[1 - par], 8 * (p1 - (1 - par) + 2))
                    if relation:
                        pool.wait_ge(o_res_ready, done(p3))
                    pool.tensor_tensor(xb[:, 1 - par], x0[:, 1 - par], both(beta_ln_bc), ALU.add).then_inc(xb_ready, 1)
                if relation:
                    wait_before(pool, z_ready[1], p3)
                    inverse_root(1, p3, done(p3, 2))
                if last_layer:
                    pool.wait_ge(x3_ready, done(p5))
                    wait_before(pool, x4_ready, p5)
                    pool.tensor_tensor(x3b[:], x3_up[:, 1 - par], both(b_out_less), ALU.add).then_inc(x3b_ready, 1)
                if gat:
                    pool.wait_ge(e_leaky_ready, done(p4))
                    pool.tensor_tensor(e_mask[:], e_leaky[:], both(adj_sb), ALU.mult).then_inc(e_mask_ready, 1)
                if entry:
                    wait_before(pool, z_ready[0], p0)
                    inverse_root(0, p0, done(p0, 2))
                if relation:
                    pool.wait_ge(rel_ready, done(p3))
                    wait_before(pool, sum_sq_psum, p3)
                    pool.tensor_tensor(rel_sq[:], rel[:], rel[:], ALU.mult).then_inc(rel_sq_ready, 1)
                    pool.wait_ge(sum_sq_ready, done(p3))
                    wait_before(pool, x2_ready, p3, 2)
                    pool.tensor_tensor(inv_norm[:], sum_sq[:], minus_half[:], ALU.pow).then_inc(inv_norm_ready, 1)
                if gat:
                    wait_before(pool, h3_ready, p4)
                    inverse_root(3, p4, done(p4, 2))
                if relation:
                    wait_before(pool, z_ready[2], p3)
                    inverse_root(2, p3, done(p3, 2))

            run(pool, step, {0: wait_for_constants, 1: split_weights})


def kernel(**inputs):
    import concourse.bacc as bacc
    from concourse.bass_utils import run_bass_kernel_spmd

    def laid(a):
        return np.ascontiguousarray(np.asarray(a))

    arrays = {
        "x": laid(inputs["x"]),
        "adj": laid(inputs["adj"]),
        "adj_t": laid(np.asarray(inputs["adj"]).T),
        "w_qkv": laid(inputs["L0_gnn_w_qkv"]),
        "w_proj": laid(inputs["L0_gnn_w_proj"]),
        "b_proj": laid(inputs["L0_gnn_b_proj"]),
        "gamma": laid(inputs["L0_gnn_ln_gamma"]),
        "beta_ln": laid(inputs["L0_gnn_ln_beta"]),
        "w_q": laid(inputs["L1_gnn_Wq"]),
        "w_k": laid(inputs["L1_gnn_Wk"]),
        "w_v_t": laid(np.asarray(inputs["L1_gnn_Wv"]).T),
        "w_gat": laid(inputs["L2_gnn_W"]),
        "a_gat": laid(np.asarray(inputs["L2_gnn_a"]).reshape(2, -1)),
        "beta_gat": laid(inputs["L2_gnn_beta"]),
        "w_out": laid(inputs["L3_gnn_weight"]),
        "b_out": laid(inputs["L3_gnn_bias"]),
    }
    nc = bacc.Bacc("TRN2", target_bir_lowering=False, num_devices=1)
    args = [nc.dram_tensor(f"in_{k}", a.shape, mybir.dt.from_np(a.dtype), kind="ExternalInput").ap()
            for k, a in arrays.items()]
    out = nc.dram_tensor("out_x", arrays["x"].shape, mybir.dt.float32, kind="ExternalOutput").ap()
    order = ["x", "adj", "adj_t", "w_qkv", "w_proj", "b_proj", "gamma", "beta_ln", "w_q", "w_k", "w_v_t",
             "w_gat", "a_gat", "beta_gat", "w_out", "b_out"]
    at = dict(zip(arrays, args))
    gnn_stack(nc, *[at[k] for k in order], out)
    r = run_bass_kernel_spmd(nc, [{f"in_{k}": a for k, a in arrays.items()}], core_ids=[0])
    return r.results[0]["out_x"]
```
